# Optimizing a Trainium2 kernel written in Bass

```python
import numpy as np
import jax
import jax.numpy as jnp

def _softmax(x, axis=-1):
    return jax.nn.softmax(x, axis=axis)

def _gelu(x):
    return jax.nn.gelu(x, approximate=True)

def _silu(x):
    return jax.nn.silu(x)

def _sigmoid(x):
    return jax.nn.sigmoid(x)

def _layernorm(x, axis=-1, eps=1e-05):
    m = jnp.mean(x, axis=axis, keepdims=True)
    v = jnp.var(x, axis=axis, keepdims=True)
    return (x - m) / jnp.sqrt(v + eps)

def _scatter_add(tgt, idx, src, axis=0):
    return tgt.at[idx].add(src)

def _segment_sum(src, seg, n):
    return jax.ops.segment_sum(src, seg, n)
kernel_name = 'mk_dlrm_tower_d1_rec_r8_e31aaa'

def setup_inputs(seed: int=0):
    np.random.seed(seed)
    _w = jnp.asarray

    def _rec_inputs():
        import jax
        import jax.numpy as jnp
        _tk = jax.random.key(seed)
        dense_ctx = jax.random.normal(jax.random.fold_in(_tk, 190), (512, 16), jnp.float32)
        ids = jnp.stack([jax.random.randint(jax.random.fold_in(_tk, 200 + f), (512,), 0, v, jnp.int32) for f, v in enumerate([125000, 12500, 125000, 125000, 125000, 1250, 1250, 1250, 1000, 1000, 1000, 12500, 1250, 125000, 1250, 125000, 1250, 125000, 125000, 1000, 1000, 1250, 12500, 1000, 12500, 12500, 1250, 125000, 12500, 1000, 12500, 1250])], axis=1)
        tbl_0 = 0.05 * jax.random.normal(jax.random.fold_in(_tk, 500 + 0), (125000, 16), jnp.float32)
        tbl_1 = 0.05 * jax.random.normal(jax.random.fold_in(_tk, 500 + 1), (12500, 16), jnp.float32)
        tbl_2 = 0.05 * jax.random.normal(jax.random.fold_in(_tk, 500 + 2), (125000, 16), jnp.float32)
        tbl_3 = 0.05 * jax.random.normal(jax.random.fold_in(_tk, 500 + 3), (125000, 16), jnp.float32)
        tbl_4 = 0.05 * jax.random.normal(jax.random.fold_in(_tk, 500 + 4), (125000, 16), jnp.float32)
        tbl_5 = 0.05 * jax.random.normal(jax.random.fold_in(_tk, 500 + 5), (1250, 16), jnp.float32)
        tbl_6 = 0.05 * jax.random.normal(jax.random.fold_in(_tk, 500 + 6), (1250, 16), jnp.float32)
        tbl_7 = 0.05 * jax.random.normal(jax.random.fold_in(_tk, 500 + 7), (1250, 16), jnp.float32)
        tbl_8 = 0.05 * jax.random.normal(jax.random.fold_in(_tk, 500 + 8), (1000, 16), jnp.float32)
        tbl_9 = 0.05 * jax.random.normal(jax.random.fold_in(_tk, 500 + 9), (1000, 16), jnp.float32)
        tbl_10 = 0.05 * jax.random.normal(jax.random.fold_in(_tk, 500 + 10), (1000, 16), jnp.float32)
        tbl_11 = 0.05 * jax.random.normal(jax.random.fold_in(_tk, 500 + 11), (12500, 16), jnp.float32)
        tbl_12 = 0.05 * jax.random.normal(jax.random.fold_in(_tk, 500 + 12), (1250, 16), jnp.float32)
        tbl_13 = 0.05 * jax.random.normal(jax.random.fold_in(_tk, 500 + 13), (125000, 16), jnp.float32)
        tbl_14 = 0.05 * jax.random.normal(jax.random.fold_in(_tk, 500 + 14), (1250, 16), jnp.float32)
        tbl_15 = 0.05 * jax.random.normal(jax.random.fold_in(_tk, 500 + 15), (125000, 16), jnp.float32)
        tbl_16 = 0.05 * jax.random.normal(jax.random.fold_in(_tk, 500 + 16), (1250, 16), jnp.float32)
        tbl_17 = 0.05 * jax.random.normal(jax.random.fold_in(_tk, 500 + 17), (125000, 16), jnp.float32)
        tbl_18 = 0.05 * jax.random.normal(jax.random.fold_in(_tk, 500 + 18), (125000, 16), jnp.float32)
        tbl_19 = 0.05 * jax.random.normal(jax.random.fold_in(_tk, 500 + 19), (1000, 16), jnp.float32)
        tbl_20 = 0.05 * jax.random.normal(jax.random.fold_in(_tk, 500 + 20), (1000, 16), jnp.float32)
        tbl_21 = 0.05 * jax.random.normal(jax.random.fold_in(_tk, 500 + 21), (1250, 16), jnp.float32)
        tbl_22 = 0.05 * jax.random.normal(jax.random.fold_in(_tk, 500 + 22), (12500, 16), jnp.float32)
        tbl_23 = 0.05 * jax.random.normal(jax.random.fold_in(_tk, 500 + 23), (1000, 16), jnp.float32)
        tbl_24 = 0.05 * jax.random.normal(jax.random.fold_in(_tk, 500 + 24), (12500, 16), jnp.float32)
        tbl_25 = 0.05 * jax.random.normal(jax.random.fold_in(_tk, 500 + 25), (12500, 16), jnp.float32)
        tbl_26 = 0.05 * jax.random.normal(jax.random.fold_in(_tk, 500 + 26), (1250, 16), jnp.float32)
        tbl_27 = 0.05 * jax.random.normal(jax.random.fold_in(_tk, 500 + 27), (125000, 16), jnp.float32)
        tbl_28 = 0.05 * jax.random.normal(jax.random.fold_in(_tk, 500 + 28), (12500, 16), jnp.float32)
        tbl_29 = 0.05 * jax.random.normal(jax.random.fold_in(_tk, 500 + 29), (1000, 16), jnp.float32)
        tbl_30 = 0.05 * jax.random.normal(jax.random.fold_in(_tk, 500 + 30), (12500, 16), jnp.float32)
        tbl_31 = 0.05 * jax.random.normal(jax.random.fold_in(_tk, 500 + 31), (1250, 16), jnp.float32)
        _rk = jax.random.fold_in(_tk, 7)
        W_top1 = 0.0693375 * jax.random.normal(jax.random.fold_in(_tk, 801), (208, 512), jnp.float32)
        W_top2 = 0.0441942 * jax.random.normal(jax.random.fold_in(_tk, 802), (512, 256), jnp.float32)
        W_top3 = 0.0625 * jax.random.normal(jax.random.fold_in(_tk, 803), (256, 1), jnp.float32)
        b_top1 = jnp.zeros((512,), jnp.float32)
        b_top2 = jnp.zeros((256,), jnp.float32)
        return (dense_ctx, ids, tbl_0, tbl_1, tbl_2, tbl_3, tbl_4, tbl_5, tbl_6, tbl_7, tbl_8, tbl_9, tbl_10, tbl_11, tbl_12, tbl_13, tbl_14, tbl_15, tbl_16, tbl_17, tbl_18, tbl_19, tbl_20, tbl_21, tbl_22, tbl_23, tbl_24, tbl_25, tbl_26, tbl_27, tbl_28, tbl_29, tbl_30, tbl_31, W_top1, b_top1, W_top2, b_top2, W_top3)
    dense_ctx, ids, tbl_0, tbl_1, tbl_2, tbl_3, tbl_4, tbl_5, tbl_6, tbl_7, tbl_8, tbl_9, tbl_10, tbl_11, tbl_12, tbl_13, tbl_14, tbl_15, tbl_16, tbl_17, tbl_18, tbl_19, tbl_20, tbl_21, tbl_22, tbl_23, tbl_24, tbl_25, tbl_26, tbl_27, tbl_28, tbl_29, tbl_30, tbl_31, W_top1, b_top1, W_top2, b_top2, W_top3 = _rec_inputs()

    def _L0_rec_setup():
        import jax, jax.numpy as jnp
        import numpy as np
        B, M, D = (2048, 32, 16)
        LAYERS = [64, 64, 64]
        key = jax.random.key(seed)
        ks = jax.random.split(key, 4)
        inp = {'embeddings': jax.random.normal(ks[0], (B, M, D), dtype=jnp.float32)}
        hk_1 = M
        for i, hk in enumerate(LAYERS):
            scale = (2.0 / (M * hk_1 + hk)) ** 0.5
            inp[f'W{i}'] = jax.random.normal(ks[i + 1], (M, hk_1, hk), dtype=jnp.float32) * scale
            hk_1 = hk
        return inp
    _L0_rec_all = _L0_rec_setup()
    _L0_rec_in = {k: v for k, v in _L0_rec_all.items() if k in ('W0', 'W1', 'W2')}
    del _L0_rec_all
    return {'dense_ctx': dense_ctx, 'ids': ids, 'tbl_0': tbl_0, 'tbl_1': tbl_1, 'tbl_2': tbl_2, 'tbl_3': tbl_3, 'tbl_4': tbl_4, 'tbl_5': tbl_5, 'tbl_6': tbl_6, 'tbl_7': tbl_7, 'tbl_8': tbl_8, 'tbl_9': tbl_9, 'tbl_10': tbl_10, 'tbl_11': tbl_11, 'tbl_12': tbl_12, 'tbl_13': tbl_13, 'tbl_14': tbl_14, 'tbl_15': tbl_15, 'tbl_16': tbl_16, 'tbl_17': tbl_17, 'tbl_18': tbl_18, 'tbl_19': tbl_19, 'tbl_20': tbl_20, 'tbl_21': tbl_21, 'tbl_22': tbl_22, 'tbl_23': tbl_23, 'tbl_24': tbl_24, 'tbl_25': tbl_25, 'tbl_26': tbl_26, 'tbl_27': tbl_27, 'tbl_28': tbl_28, 'tbl_29': tbl_29, 'tbl_30': tbl_30, 'tbl_31': tbl_31, 'W_top1': W_top1, 'b_top1': b_top1, 'W_top2': W_top2, 'b_top2': b_top2, 'W_top3': W_top3, 'L0_rec_W0': _L0_rec_in['W0'], 'L0_rec_W1': _L0_rec_in['W1'], 'L0_rec_W2': _L0_rec_in['W2']}

def reference(dense_ctx, ids, tbl_0, tbl_1, tbl_2, tbl_3, tbl_4, tbl_5, tbl_6, tbl_7, tbl_8, tbl_9, tbl_10, tbl_11, tbl_12, tbl_13, tbl_14, tbl_15, tbl_16, tbl_17, tbl_18, tbl_19, tbl_20, tbl_21, tbl_22, tbl_23, tbl_24, tbl_25, tbl_26, tbl_27, tbl_28, tbl_29, tbl_30, tbl_31, W_top1, b_top1, W_top2, b_top2, W_top3, L0_rec_W0, L0_rec_W1, L0_rec_W2):
    import jax
    import jax.numpy as jnp

    def _L0_rec_ref(embeddings, W0, W1, W2):
        import jax, jax.numpy as jnp
        import numpy as np
        B, M, D = (2048, 32, 16)
        LAYERS = [64, 64, 64]
        x0 = embeddings
        xk = x0
        outs = []
        for W in (W0, W1, W2):
            xk = jax.nn.relu(jnp.einsum('bmd,bhd,mhk->bkd', x0, xk, W))
            outs.append(jnp.sum(xk, axis=2))
        return jnp.concatenate(outs, axis=1)
    e = jnp.stack([tbl_0[ids[:, 0]], tbl_1[ids[:, 1]], tbl_2[ids[:, 2]], tbl_3[ids[:, 3]], tbl_4[ids[:, 4]], tbl_5[ids[:, 5]], tbl_6[ids[:, 6]], tbl_7[ids[:, 7]], tbl_8[ids[:, 8]], tbl_9[ids[:, 9]], tbl_10[ids[:, 10]], tbl_11[ids[:, 11]], tbl_12[ids[:, 12]], tbl_13[ids[:, 13]], tbl_14[ids[:, 14]], tbl_15[ids[:, 15]], tbl_16[ids[:, 16]], tbl_17[ids[:, 17]], tbl_18[ids[:, 18]], tbl_19[ids[:, 19]], tbl_20[ids[:, 20]], tbl_21[ids[:, 21]], tbl_22[ids[:, 22]], tbl_23[ids[:, 23]], tbl_24[ids[:, 24]], tbl_25[ids[:, 25]], tbl_26[ids[:, 26]], tbl_27[ids[:, 27]], tbl_28[ids[:, 28]], tbl_29[ids[:, 29]], tbl_30[ids[:, 30]], tbl_31[ids[:, 31]]], axis=1)
    z = _L0_rec_ref(e, L0_rec_W0, L0_rec_W1, L0_rec_W2)
    z = z.reshape(z.shape[0], -1)
    h = jnp.concatenate([z, dense_ctx], axis=1)
    h = jnp.maximum(h @ W_top1 + b_top1, 0.0)
    h = jnp.maximum(h @ W_top2 + b_top2, 0.0)
    y = h @ W_top3
    return y

_drawn_inputs = setup_inputs


def setup_inputs(seed=0):
    import zlib

    import numpy as np

    out = dict(_drawn_inputs(seed))
    spreads = {'b_top1': (0.0, 2.0), 'b_top2': (0.0, 0.8)}
    factors = {'tbl_0': 8.0,
     'tbl_1': 8.0,
     'tbl_2': 8.0,
     'tbl_3': 8.0,
     'tbl_4': 8.0,
     'tbl_5': 8.0,
     'tbl_6': 8.0,
     'tbl_7': 8.0,
     'tbl_8': 8.0,
     'tbl_9': 8.0,
     'tbl_10': 8.0,
     'tbl_11': 8.0,
     'tbl_12': 8.0,
     'tbl_13': 8.0,
     'tbl_14': 8.0,
     'tbl_15': 8.0,
     'tbl_16': 8.0,
     'tbl_17': 8.0,
     'tbl_18': 8.0,
     'tbl_19': 8.0,
     'tbl_20': 8.0,
     'tbl_21': 8.0,
     'tbl_22': 8.0,
     'tbl_23': 8.0,
     'tbl_24': 8.0,
     'tbl_25': 8.0,
     'tbl_26': 8.0,
     'tbl_27': 8.0,
     'tbl_28': 8.0,
     'tbl_29': 8.0,
     'tbl_30': 8.0,
     'tbl_31': 8.0,
     'L0_rec_W0': 3.652,
     'L0_rec_W1': 8.0,
     'L0_rec_W2': 8.0,
     'dense_ctx': 7.636}
    for name, (base, spread) in spreads.items():
        noise = np.random.default_rng([zlib.crc32(name.encode()), seed]).standard_normal(out[name].shape)
        drawn = base * np.exp(spread * noise) if base else spread * noise
        out[name] = jnp.asarray(drawn.astype(out[name].dtype))
    for name, factor in factors.items():
        out[name] = (out[name] * factor).astype(out[name].dtype)
    return out
```

```python
from contextlib import ExitStack

import numpy as np
import concourse.bass as bass
from concourse import mybir

F32 = mybir.dt.float32
I32 = mybir.dt.int32
ALU = mybir.AluOpType
ACT = mybir.ActivationFunctionType

P = 128
M = 32
D = 16
K = 64
TILE = 512
PAIR = 2 * TILE
DP = PAIR // P
NC = M * K // P
GC = 2
NG = NC // GC
LC = 4
NL = NC // LC
N0 = M // 8
HALF = M // 2
H1 = 512
H2 = 256


def build(nc, dense_t, ids, tables, w0_fwd, w0_bwd, w1, w2, w_top1, b_top1, w_top2, b_top2, w_top3, eye, y):
    B = ids.shape[0]
    NB = B // P
    NP = 2 * NB
    ND = dense_t.shape[0]
    C1 = H1 // P
    C2 = H2 // P
    NZ = 3

    x0_dram = nc.dram_tensor("x0_scratch", (NP, 2 * M, PAIR), F32, kind="Internal").ap()

    with ExitStack() as ctx:
        def sb(name, shape, dt=F32):
            return ctx.enter_context(nc.sbuf_tensor(name, shape, dt))

        def psum(name, shape):
            return ctx.enter_context(nc.psum_tensor(name, shape, F32))

        def sem(name):
            return ctx.enter_context(nc.semaphore(name))

        ids_sb = sb("ids_sb", [P, NB, M], I32)
        gath = sb("gath", [P, M * D])
        ident = sb("ident", [P, P])
        x0rep = [sb(f"x0rep{q}", [P, PAIR]) for q in range(2)]
        rot = sb("rot", [P, N0 + 1, PAIR])
        x0bc = [sb(f"x0bc{q}", [P, NC, PAIR]) for q in range(2)]
        ring = sb("ring", [P, 2, GC, PAIR])
        w0_sb = sb("w0_sb", [P, N0 + 1, K])
        w1_sb = sb("w1_sb", [P, NC, K])
        w2_sb = sb("w2_sb", [P, NC, K])
        wt1_sb = sb("wt1_sb", [P, NZ, H1])
        wt2_sb = sb("wt2_sb", [P, C1, H2])
        wt3_sb = sb("wt3_sb", [P, C2])
        bt1_sb = sb("bt1_sb", [P, C1])
        bt2_sb = sb("bt2_sb", [P, C2])
        relu_z = [sb(f"relu_z{l}", [P, TILE]) for l in range(NZ)]
        z = [sb(f"z{l}", [P, P]) for l in range(NZ)]
        h1 = sb("h1", [P, C1, P])
        h2 = sb("h2", [P, C2, P])
        y_sb = sb("y_sb", [P, NB])
        dense_sb = rot[32:32 + ND, N0, 0:P]
        wdense_sb = rot[32:32 + ND, N0, TILE:TILE + H1]
        w0_bwd_sb = ring[:, 0, 0, 0:(N0 + 1) * K].rearrange("p (c k) -> p c k", k=K)

        acc = [psum(f"acc{n}", [P, TILE]) for n in range(2)]
        x1_ps = psum("x1_ps", [P, PAIR])
        x2_ps = psum("x2_ps", [P, PAIR])
        aux = psum("aux", [P, PAIR])

        ids_in = sem("ids_in")
        ident_in = sem("ident_in")
        w0_in = sem("w0_in")
        w0b_in = sem("w0b_in")
        w1_in = sem("w1_in")
        w2_in = sem("w2_in")
        mlp_in = sem("mlp_in")
        dense_in = sem("dense_in")
        w0_sym = sem("w0_sym")
        gathered = sem("gathered")
        transposed = sem("transposed")
        x0rows_ready = sem("x0rows_ready")
        x0rep_ready = sem("x0rep_ready")
        x0_stored = [sem(f"x0_stored{q}") for q in range(2)]
        rot_in = sem("rot_in")
        bc_in = [[sem(f"bc_in{q}_{g}") for g in range(NL)] for q in range(2)]
        p0_dve = sem("p0_dve")
        p0_pool = sem("p0_pool")
        p1_ready = sem("p1_ready")
        p2_ready = sem("p2_ready")
        p0_used = sem("p0_used")
        p1_used = sem("p1_used")
        p2_used = sem("p2_used")
        x1_ready = sem("x1_ready")
        x2_ready = sem("x2_ready")
        acc_read = sem("acc_read")
        z_step = sem("z_step")
        z_added = [sem(f"z_added{l}") for l in range(NZ)]
        h1_mm = sem("h1_mm")
        h1_ready = sem("h1_ready")
        h2_mm = sem("h2_mm")
        h2_ready = sem("h2_ready")
        y_mm = sem("y_mm")
        y_ready = sem("y_ready")
        y_out = sem("y_out")

        DVE0_FIRST = 3
        POOL0 = 3

        def p0_dve_count(pair, first):
            if isinstance(pair, int) and pair < 2:
                return DVE0_FIRST * pair + (1 if first else DVE0_FIRST)
            return 2 * DVE0_FIRST + (pair - 2) + 1

        block = ctx.enter_context(nc.Block())

        @block.sync
        def _(sp):
            SLOT = 2 * M * PAIR

            def store_x0(q, base, rows_ready):
                sp.wait_ge(x0rows_ready, rows_ready)
                dst = bass.AP(x0_dram.tensor, base, [[PAIR, 2 * M], [1, PAIR]])
                sp.dma_start(dst, x0rep[q][0:2 * M, :]).then_inc(x0_stored[q], 16)

            def load_rot(q, base, stored, used):
                sp.wait_ge(x0_stored[q], stored)
                if used is not None:
                    sp.wait_ge(p0_used, used)
                for jj in range(4):
                    src = bass.AP(x0_dram.tensor, base + jj * PAIR, [[PAIR, M], [4 * PAIR, N0], [1, PAIR]])
                    sp.dma_start(rot[M * jj:M * jj + M, 0:N0, :], src).then_inc(rot_in, 16)
                src = bass.AP(x0_dram.tensor, base + HALF * PAIR, [[PAIR, HALF], [1, PAIR]])
                sp.dma_start(rot[0:HALF, N0, :], src).then_inc(rot_in, 16)

            def load_bc(q, g, base):
                for half in range(2):
                    src = bass.AP(x0_dram.tensor, base + (2 * LC * g + half) * PAIR,
                                  [[0, P // 2], [2 * PAIR, LC], [1, PAIR]])
                    sp.dma_start(x0bc[q][64 * half:64 * half + 64, LC * g:LC * g + LC, :],
                                 src).then_inc(bc_in[q][g], 16)

            def load_dense(col):
                sp.dma_start(dense_sb, dense_t[:, bass.ds(col, P)]).then_inc(dense_in, 16)

            def next_block(i):
                if i >= 1:
                    sp.wait_ge(h1_mm, i)
                load_dense(i * P)
                for q in range(2):
                    pair = 2 * (i + 1) + q
                    store_x0(q, pair * SLOT, pair + 1)
                for q in range(2):
                    pair = 2 * (i + 1) + q
                    load_rot(q, pair * SLOT, 16 * (i + 2), pair)
                    for g in range(NL):
                        sp.wait_ge(p2_used, NL * (pair - 2) + g + 1)
                        load_bc(q, g, pair * SLOT)

            sp.dma_start(ids_sb[:], ids.rearrange("(t p) f -> p t f", p=P)).then_inc(ids_in, 16)
            sp.dma_start(ident[:], eye).then_inc(ident_in, 16)
            sp.dma_start(w0_sb[:], w0_fwd).then_inc(w0_in, 16)
            sp.dma_start(w0_bwd_sb, w0_bwd).then_inc(w0b_in, 16)
            sp.dma_start(w1_sb[:], w1.rearrange("(c a) h k -> (a h) c k", a=2)).then_inc(w1_in, 16)
            sp.dma_start(w2_sb[:], w2.rearrange("(c a) h k -> (a h) c k", a=2)).then_inc(w2_in, 16)
            for half in range(2):
                sp.dma_start(wt1_sb[64 * half:64 * half + 64, :, :],
                             w_top1[0:NZ * K, :].rearrange("(l k) n -> k l n", k=K)).then_inc(mlp_in, 16)
            sp.dma_start(wdense_sb, w_top1[NZ * K:NZ * K + ND, :]).then_inc(mlp_in, 16)
            sp.dma_start(wt2_sb[:], w_top2.rearrange("(c p) n -> p c n", p=P)).then_inc(mlp_in, 16)
            sp.dma_start(wt3_sb[:], w_top3).then_inc(mlp_in, 16)
            sp.dma_start(bt1_sb[:], b_top1).then_inc(mlp_in, 16)
            sp.dma_start(bt2_sb[:], b_top2).then_inc(mlp_in, 16)

            for q in range(2):
                store_x0(q, q * SLOT, q + 1)
                load_rot(q, q * SLOT, 16, q or None)
                for g in range(NL):
                    load_bc(q, g, q * SLOT)
            for i in range(NB - 1):
                next_block(i)
            sp.wait_ge(h1_mm, NB - 1)
            load_dense((NB - 1) * P)

        @block.gpsimd
        def _(pool):
            gathers = [(t, f) for t in range(NB) for f in range(M)]
            steps = [0]

            def gather(n):
                for t, f in gathers[:n]:
                    if f == 0 and t >= 1:
                        pool.wait_ge(transposed, 2 * t)
                    pool.indirect_dma_start(
                        out=gath[:, D * f:D * f + D], out_offset=None, in_=tables[f],
                        in_offset=bass.IndirectOffsetOnAxis(ap=ids_sb[:, t, f:f + 1], axis=0),
                    ).then_inc(gathered, 16)
                del gathers[:n]

            def add(out, a, b, then):
                nc.gpsimd.tensor_tensor(out, a, b, ALU.add).then_inc(then, 1)

            def sum_z(l, q, unit):
                r = relu_z[l]
                pool.wait_ge(acc_read, unit + 1)
                add(r[:, 0:256], r[:, 0:256], r[:, 256:512], z_step)
                steps[0] += 1
                pool.wait_ge(z_step, steps[0])
                if q == 0:
                    add(z[l][:], r[:, 0:128], r[:, 128:256], z_added[l])
                else:
                    add(r[:, 0:128], r[:, 0:128], r[:, 128:256], z_step)
                    steps[0] += 1
                    pool.wait_ge(z_step, steps[0])
                    add(z[l][:], z[l][:], r[:, 0:128], z_added[l])

            def layer0(pair):
                pool.wait_ge(x0rep_ready, pair + 1)
                pool.wait_ge(rot_in, 80 * (pair + 1))
                xr = x0rep[pair % 2]
                for c in (2, 3):
                    nc.gpsimd.tensor_tensor(rot[:, c, :], xr[:], rot[:, c, :], ALU.mult).then_inc(p0_pool, 1)
                nc.gpsimd.tensor_tensor(rot[0:HALF, N0, :], xr[0:HALF, :], rot[0:HALF, N0, :],
                                        ALU.mult).then_inc(p0_pool, 1)

            pool.wait_ge(ids_in, 16)
            gather(M)
            gather(M)
            for p in range(NP):
                i, q = divmod(p, 2)
                if p >= 2 and q == 0:
                    gather(6)
                if p >= 1:
                    sum_z(2, 1 - q, 3 * p)
                if 1 <= p < NP - 1:
                    layer0(p + 1)
                if q == 0 and i >= 1:
                    pool.wait_ge(h1_mm, i)
                sum_z(0, q, 3 * p - 1 if p else 0)
                if q == 1:
                    gather(26)
                sum_z(1, q, 3 * p + 1)
            sum_z(2, 1, 3 * NP - 1)

        @block.scalar
        def _(act):
            def spread(bank, x_ps, ready):
                for t in range(2):
                    for half in range(2):
                        last = nc.scalar.activation(x_ps[64 * half:64 * half + 64, TILE * t:TILE * t + TILE],
                                                    bank[64 * t:64 * t + 64, :], ACT.Relu)
                last.then_inc(ready, 1)

            def keep_z(bank, l):
                nc.scalar.activation(relu_z[l][:], bank[:], ACT.Relu).then_inc(acc_read, 1)

            def copy_x0(pair, q):
                act.wait_ge(transposed, pair + 1)
                for r, ready in enumerate((None, x0rows_ready, None, x0rep_ready)):
                    last = nc.scalar.activation(x0rep[q][M * r:M * r + M, :], aux[0:M, :], ACT.Copy)
                    if ready is not None:
                        last.then_inc(ready, 1)

            def finish_h1(block_):
                act.wait_ge(h1_mm, block_ + 1)
                for c in range(C1):
                    last = nc.scalar.activation(h1[:, c, :], aux[:, P * c:P * c + P], ACT.Relu,
                                                bias=bt1_sb[:, c:c + 1])
                last.then_inc(h1_ready, 1)

            def finish_h2(block_):
                act.wait_ge(h2_mm, block_ + 1)
                for c in range(C2):
                    last = nc.scalar.activation(h2[:, c, :], aux[:, TILE + P * c:TILE + P * c + P], ACT.Relu,
                                                bias=bt2_sb[:, c:c + 1])
                last.then_inc(h2_ready, 1)

            def finish_y(block_):
                act.wait_ge(y_mm, block_ + 1)
                nc.scalar.activation(y_sb[:, bass.ds(block_, 1)], aux[:, TILE + 256:TILE + 257], ACT.Copy).then_inc(y_ready, 1)
                act.wait_ge(y_ready, block_ + 1)
                act.dma_start(y[bass.ds(block_ * P, P), :], y_sb[:, bass.ds(block_, 1)]).then_inc(y_out, 16)

            def two_pairs(i, first, last):
                for q in range(2):
                    p = 2 * i + q
                    bank, other = acc[(3 * q + 1) % 2], acc[(3 * q + 2) % 2]
                    act.wait_ge(p1_used, NG * (p + 1))
                    if not (first and q == 0):
                        act.wait_ge(p2_ready, NG * p)
                    spread(bank, x2_ps, x2_ready)
                    if not (first and q == 0):
                        act.wait_ge(z_added[1], p)
                    keep_z(bank, 1)
                    if q == 0 and not first:
                        finish_h1(i - 1)
                    if q == 1 and not first:
                        finish_y(i - 1)
                    if not (last and q == 1):
                        act.wait_ge(p0_used, p + 2)
                        act.wait_ge(p1_ready, NG * (p + 1))
                        spread(other, x1_ps, x1_ready)
                        act.wait_ge(z_added[0], p + 1)
                        keep_z(other, 0)
                    if q == 0 and not last:
                        for r in range(2):
                            act.wait_ge(p0_dve, p0_dve_count(p + r, False))
                            if not first:
                                act.wait_ge(p0_pool, POOL0 * (p + r - 1))
                            act.wait_ge(x0_stored[r], 16 * (i + 1))
                            copy_x0(p + 2 + r, r)
                    if last and q == 1:
                        bank = other
                    act.wait_ge(p2_used, NL * (p + 1))
                    if not (first and q == 0):
                        act.wait_ge(z_added[2], p)
                    keep_z(bank, 2)
                    if q == 0 and not first:
                        finish_h2(i - 1)

            copy_x0(0, 0)
            copy_x0(1, 1)
            act.wait_ge(p0_used, 1)
            spread(acc[0], x1_ps, x1_ready)
            keep_z(acc[0], 0)
            act.wait_ge(mlp_in, 7 * 16)
            two_pairs(0, True, False)
            with act.Fori(1, NB - 1) as i:
                two_pairs(i, False, False)
            two_pairs(NB - 1, False, True)
            finish_h1(NB - 1)
            finish_h2(NB - 1)
            finish_y(NB - 1)
            act.wait_ge(y_out, 16 * NB)

        @block.vector
        def _(dve):
            def layer0(pair, q, every):
                dve.wait_ge(x0rep_ready, pair + 1)
                dve.wait_ge(rot_in, 80 * (pair + 1))
                xr = x0rep[q]
                pairs_of_chunks = (0, 2) if every else (0,)
                for c in pairs_of_chunks:
                    nc.vector.tensor_tensor(rot[:, c:c + 2, :], xr[:].unsqueeze(1).broadcast_to([P, 2, PAIR]),
                                            rot[:, c:c + 2, :], ALU.mult).then_inc(p0_dve, 1)
                if every:
                    nc.vector.tensor_tensor(rot[0:HALF, N0, :], xr[0:HALF, :], rot[0:HALF, N0, :],
                                            ALU.mult).then_inc(p0_dve, 1)

            x1_bc = x1_ps[:].unsqueeze(1).broadcast_to([P, GC, PAIR])
            x2_bc = x2_ps[:].unsqueeze(1).broadcast_to([P, GC, PAIR])

            def two_pairs(i, first, last):
                for q in range(2):
                    p = 2 * i + q
                    dve.wait_ge(x1_ready, p + 1)
                    for g in range(NG):
                        if g % 2 == 0:
                            dve.wait_ge(bc_in[q][g * GC // LC], 32 * (i + 1))
                        if not (first and q == 0 and g < 2):
                            dve.wait_ge(p1_used, NG * p + g - 1)
                        nc.vector.tensor_tensor(ring[:, g % 2, :, :], x0bc[q][:, GC * g:GC * g + GC, :], x1_bc,
                                                ALU.mult).then_inc(p1_ready, 1)
                    if not (last and q == 1):
                        layer0(p + 1, 1 - q, first and q == 0)
                    dve.wait_ge(x2_ready, p + 1)
                    for g in range(NG):
                        chunk = x0bc[q][:, GC * g:GC * g + GC, :]
                        nc.vector.tensor_tensor(chunk, chunk, x2_bc, ALU.mult).then_inc(p2_ready, 1)

            dve.wait_ge(w0_in, 16)
            dve.wait_ge(w0b_in, 16)
            for rows, cs in ((slice(M, 2 * M), slice(0, 1)), (slice(2 * M, P), slice(0, 1)), (slice(0, P), slice(1, N0)), (slice(0, HALF), slice(N0, N0 + 1))):
                last = nc.vector.tensor_tensor(w0_sb[rows, cs, :], w0_sb[rows, cs, :], w0_bwd_sb[rows, cs, :], ALU.add)
            last.then_inc(w0_sym, 1)
            dve.wait_ge(w0_sym, 1)
            layer0(0, 0, True)
            two_pairs(0, True, False)
            with dve.Fori(1, NB - 1) as i:
                two_pairs(i, False, False)
            two_pairs(NB - 1, False, True)

        @block.tensor
        def _(pe):
            def both(bank, w, prod, start, stop):
                for t in range(2):
                    last = nc.tensor.matmul(bank[64 * t:64 * t + 64, :], w, prod[:, TILE * t:TILE * t + TILE],
                                            start=start, stop=stop)
                return last

            def transpose_x0(q):
                g = gath[:].rearrange("p (m d) -> p m d", d=D)
                for dd in range(DP):
                    last = nc.tensor.transpose(aux[0:M, P * dd:P * dd + P], g[:, :, DP * q + dd], ident[:])
                last.then_inc(transposed, 1)

            def layer0(pair, bank, every):
                for c in range(N0):
                    if c == 0:
                        pe.wait_ge(p0_dve, p0_dve_count(pair, True))
                    if c == 2 and every:
                        pe.wait_ge(p0_dve, DVE0_FIRST * pair + 2)
                    if c >= 2 and not every:
                        pe.wait_ge(p0_pool, POOL0 * (pair - 2) + c - 1)
                    both(bank, w0_sb[:, c, :], rot[:, c, :], c == 0, False)
                if every:
                    pe.wait_ge(p0_dve, DVE0_FIRST * pair + 3)
                else:
                    pe.wait_ge(p0_pool, POOL0 * (pair - 1))
                both(bank, w0_sb[0:HALF, N0, :], rot[0:HALF, N0, :], False, True).then_inc(p0_used, 1)

            def mlp_h1(block_):
                for l in range(NZ):
                    pe.wait_ge(z_added[l], 2 * (block_ + 1))
                pe.wait_ge(dense_in, 16 * (block_ + 1))
                for c in range(C1):
                    out = aux[:, P * c:P * c + P]
                    for l in range(NZ):
                        nc.tensor.matmul(out, wt1_sb[:, l, P * c:P * c + P], z[l][:], start=(l == 0), stop=False)
                    last = nc.tensor.matmul(out, wdense_sb[:, P * c:P * c + P], dense_sb,
                                            start=False, stop=True)
                last.then_inc(h1_mm, 1)

            def mlp_h2(block_):
                pe.wait_ge(h1_ready, block_ + 1)
                for n in range(C2):
                    for c in range(C1):
                        last = nc.tensor.matmul(aux[:, TILE + P * n:TILE + P * n + P], wt2_sb[:, c, P * n:P * n + P],
                                                h1[:, c, :], start=(c == 0), stop=(c == C1 - 1))
                last.then_inc(h2_mm, 1)

            def mlp_y(block_):
                pe.wait_ge(h2_ready, block_ + 1)
                for c in range(C2):
                    last = nc.tensor.matmul(aux[:, TILE + 256:TILE + 257], h2[:, c, :], wt3_sb[:, c:c + 1],
                                            start=(c == 0), stop=(c == C2 - 1))
                last.then_inc(y_mm, 1)

            def two_pairs(i, first, last):
                for q in range(2):
                    p = 2 * i + q
                    bank, other = acc[(3 * q + 1) % 2], acc[(3 * q + 2) % 2]
                    if not (first and q == 0):
                        pe.wait_ge(acc_read, 3 * p)
                    for g in range(NG):
                        pe.wait_ge(p1_ready, NG * p + g + 1)
                        for c in range(GC):
                            done = both(bank, w1_sb[:, GC * g + c, :], ring[:, g % 2, c, :],
                                        g == 0 and c == 0, g == NG - 1 and c == GC - 1)
                        done.then_inc(p1_used, 1)
                    if q == 0 and not first:
                        pe.wait_ge(x0rep_ready, 2 * i + 2)
                        mlp_h1(i - 1)
                    if q == 1 and not first:
                        mlp_y(i - 1)
                    if not (last and q == 1):
                        pe.wait_ge(acc_read, 3 * p + 1)
                        layer0(p + 1, other, first and q == 0)
                    if last and q == 1:
                        bank = other
                    pe.wait_ge(acc_read, 3 * p + 2 - (1 if last and q == 1 else 0))
                    for g in range(NG):
                        if g == NG // 2 and q == 0 and not last:
                            pe.wait_ge(gathered, 16 * M * (i + 2))
                            if not first:
                                pe.wait_ge(h1_ready, i)
                            transpose_x0(0)
                            pe.wait_ge(x0rep_ready, 2 * i + 3)
                            transpose_x0(1)
                        pe.wait_ge(p2_ready, NG * p + g + 1)
                        for c in range(GC):
                            done = both(bank, w2_sb[:, GC * g + c, :], x0bc[q][:, GC * g + c, :],
                                        g == 0 and c == 0, g == NG - 1 and c == GC - 1)
                        if (g + 1) * GC % LC == 0:
                            done.then_inc(p2_used, 1)
                    if q == 0 and not first:
                        if not last:
                            pe.wait_ge(x0rep_ready, 2 * i + 4)
                        mlp_h2(i - 1)

            pe.wait_ge(ident_in, 16)
            pe.wait_ge(gathered, 16 * M)
            transpose_x0(0)
            pe.wait_ge(x0rep_ready, 1)
            transpose_x0(1)
            pe.wait_ge(w0_sym, 1)
            layer0(0, acc[0], True)
            pe.wait_ge(w1_in, 16)
            pe.wait_ge(w2_in, 16)
            pe.wait_ge(mlp_in, 7 * 16)
            two_pairs(0, True, False)
            with pe.Fori(1, NB - 1) as i:
                two_pairs(i, False, False)
            two_pairs(NB - 1, False, True)
            mlp_h1(NB - 1)
            mlp_h2(NB - 1)
            mlp_y(NB - 1)


def layer0_rows():
    part, chunk = np.meshgrid(np.arange(P), np.arange(N0 + 1), indexing="ij")
    m = part % M
    j = 4 * chunk + part // M
    h = (m + j) % M
    return M * m + h, M * h + m


def kernel(**inputs):
    import concourse.bacc as bacc
    from concourse.bass_utils import run_bass_kernel_spmd

    fwd, bwd = layer0_rows()
    w0 = np.asarray(inputs["L0_rec_W0"]).reshape(M * M, K)
    arrays = {
        "dense_t": np.ascontiguousarray(np.asarray(inputs["dense_ctx"]).T),
        "ids": np.ascontiguousarray(inputs["ids"]),
        "w0_fwd": np.ascontiguousarray(w0[fwd]),
        "w0_bwd": np.ascontiguousarray(w0[bwd]),
        "w1": np.ascontiguousarray(inputs["L0_rec_W1"]),
        "w2": np.ascontiguousarray(inputs["L0_rec_W2"]),
        "w_top1": np.ascontiguousarray(inputs["W_top1"]),
        "b_top1": np.ascontiguousarray(np.asarray(inputs["b_top1"]).reshape(-1, P).T),
        "w_top2": np.ascontiguousarray(inputs["W_top2"]),
        "b_top2": np.ascontiguousarray(np.asarray(inputs["b_top2"]).reshape(-1, P).T),
        "w_top3": np.ascontiguousarray(np.asarray(inputs["W_top3"]).reshape(-1, P).T),
        "eye": np.eye(P, dtype=np.float32),
    }
    for f in range(M):
        arrays[f"tbl_{f}"] = np.ascontiguousarray(inputs[f"tbl_{f}"])

    nc = bacc.Bacc("TRN2", target_bir_lowering=False, num_devices=1)
    ap = {n: nc.dram_tensor(n, a.shape, mybir.dt.from_np(a.dtype), kind="ExternalInput").ap()
          for n, a in arrays.items()}
    y = nc.dram_tensor("y", (arrays["ids"].shape[0], 1), F32, kind="ExternalOutput").ap()
    build(nc, ap["dense_t"], ap["ids"], [ap[f"tbl_{f}"] for f in range(M)], ap["w0_fwd"], ap["w0_bwd"],
          ap["w1"], ap["w2"], ap["w_top1"], ap["b_top1"], ap["w_top2"], ap["b_top2"], ap["w_top3"],
          ap["eye"], y)
    r = run_bass_kernel_spmd(nc, [arrays], core_ids=[0])
    return r.results[0]["y"]
```

```python
from contextlib import ExitStack

import numpy as np
import concourse.bass as bass
from concourse import mybir

F32 = mybir.dt.float32
I32 = mybir.dt.int32
ALU = mybir.AluOpType
ACT = mybir.ActivationFunctionType

P = 128
M = 32
D = 16
K = 64
TILE = 512
PAIR = 2 * TILE
DP = PAIR // P
NC = M * K // P
GC = 2
NG = NC // GC
LC = 4
NL = NC // LC
RING = 4
L2_ORDER = [*range(NG - LC // GC, NG), *range(NG - LC // GC)]
N0 = M // 8
HALF = M // 2
H1 = 512
H2 = 256


def build(nc, dense_t, ids, tables, w0_fwd, w0_bwd, w1, w2, w_top1, b_top1, w_top2, b_top2, w_top3, eye, y):
    B = ids.shape[0]
    NB = B // P
    NP = 2 * NB
    ND = dense_t.shape[0]
    C1 = H1 // P
    C2 = H2 // P
    NZ = 3

    x0_dram = nc.dram_tensor("x0_scratch", (NP, M, PAIR), F32, kind="Internal").ap()

    with ExitStack() as ctx:
        def sb(name, shape, dt=F32):
            return ctx.enter_context(nc.sbuf_tensor(name, shape, dt))

        def psum(name, shape):
            return ctx.enter_context(nc.psum_tensor(name, shape, F32))

        def sem(name):
            return ctx.enter_context(nc.semaphore(name))

        ids_sb = sb("ids_sb", [P, NB, M], I32)
        gath = sb("gath", [P, M * D])
        ident = sb("ident", [P, P])
        x0rep = [sb(f"x0rep{q}", [P, PAIR]) for q in range(2)]
        rot = sb("rot", [P, N0 + 1, PAIR])
        x0bc_own = [sb(f"x0bc_own{q}", [P, NC - LC, PAIR]) for q in range(2)]
        x0bc_shared = sb("x0bc_shared", [P, LC, PAIR])
        x2_sb = sb("x2_sb", [P, PAIR])
        ring = sb("ring", [P, RING, GC, PAIR])
        w0_sb = sb("w0_sb", [P, N0 + 1, K])
        w1_sb = sb("w1_sb", [P, NC, K])
        w2_sb = sb("w2_sb", [P, NC, K])
        wt1_sb = sb("wt1_sb", [P, NZ, H1])
        wt2_sb = sb("wt2_sb", [P, C1, H2])
        wt3_sb = sb("wt3_sb", [P, C2])
        bt1_sb = sb("bt1_sb", [P, C1])
        bt2_sb = sb("bt2_sb", [P, C2])
        relu_z = [sb(f"relu_z{l}", [P, TILE]) for l in range(NZ)]
        z = [sb(f"z{l}", [P, P]) for l in range(NZ)]
        h1 = relu_z[1][:].rearrange("p (c n) -> p c n", n=P)
        h2 = relu_z[2][:, 0:C2 * P].rearrange("p (c n) -> p c n", n=P)
        y_sb = sb("y_sb", [P, NB])
        dense_sb = rot[32:32 + ND, N0, 0:P]
        wdense_sb = rot[32:32 + ND, N0, TILE:TILE + H1]
        w0_bwd_sb = ring[:, 0, 0, 0:(N0 + 1) * K].rearrange("p (c k) -> p c k", k=K)

        acc = [psum(f"acc{n}", [P, TILE]) for n in range(2)]
        x1_ps = psum("x1_ps", [P, PAIR])
        x2_ps = psum("x2_ps", [P, PAIR])
        aux = psum("aux", [P, PAIR])

        ids_in = sem("ids_in")
        ident_in = sem("ident_in")
        w0_in = sem("w0_in")
        w0b_in = sem("w0b_in")
        w1_in = sem("w1_in")
        w2_in = sem("w2_in")
        mlp_in = sem("mlp_in")
        dense_in = sem("dense_in")
        w0_sym = sem("w0_sym")
        gathered = sem("gathered")
        transposed = sem("transposed")
        x0rows_ready = sem("x0rows_ready")
        x0rep_ready = sem("x0rep_ready")
        x0_stored = [sem(f"x0_stored{q}") for q in range(2)]
        rot_in = [sem(f"rot_in{n}") for n in range(2)]
        bc_in = [[sem(f"bc_in{q}_{g}") for g in range(NL)] for q in range(2)]
        p0_dve = sem("p0_dve")
        p0_pool = sem("p0_pool")
        p1_ready = sem("p1_ready")
        p2_dve = sem("p2_dve")
        p2_pool = sem("p2_pool")
        p0_used = sem("p0_used")
        p1_used = sem("p1_used")
        p2_used = sem("p2_used")
        x1_ready = sem("x1_ready")
        x2_ready = sem("x2_ready")
        x2_sb_ready = sem("x2_sb_ready")
        acc_read = sem("acc_read")
        z_step = sem("z_step")
        z_last = sem("z_last")
        z_added = [sem(f"z_added{l}") for l in range(NZ)]
        h1_mm = sem("h1_mm")
        h1_ready = sem("h1_ready")
        h2_mm = sem("h2_mm")
        h2_ready = sem("h2_ready")
        y_mm = sem("y_mm")
        y_ready = sem("y_ready")
        y_out = sem("y_out")

        P2_POOL = (1, 4)
        T_AT = (3, 7)
        P2_DVE = NG - len(P2_POOL)

        def p0_dve_done(pair, n):
            if isinstance(pair, int) and pair < 2:
                return 3 * pair + n
            return 2 * pair + 2 + n

        def x0_chunks(q, c, n):
            if c < NC - LC:
                return x0bc_own[q][:, c:c + n, :]
            return x0bc_shared[:, c - (NC - LC):c - (NC - LC) + n, :]

        block = ctx.enter_context(nc.Block())

        @block.sync
        def _(sp):
            SLOT = M * PAIR

            def store_x0(q, base, rows_ready):
                sp.wait_ge(x0rows_ready, rows_ready)
                dst = bass.AP(x0_dram.tensor, base, [[PAIR, M], [1, PAIR]])
                sp.dma_start(dst, x0rep[q][0:M, :]).then_inc(x0_stored[q], 16)

            def load_rot(q, rows_ready, used):
                sp.wait_ge(x0rows_ready, rows_ready)
                if used is not None:
                    sp.wait_ge(p0_used, used)
                for c in range(N0):
                    for jj in range(4):
                        sp.dma_start(rot[M * jj:M * jj + M, c, :],
                                     x0rep[q][4 * c + jj:4 * c + jj + M, :]).then_inc(rot_in[c // 2], 16)
                sp.dma_start(rot[0:HALF, N0, :], x0rep[q][HALF:M, :]).then_inc(rot_in[1], 16)

            def load_bc(q, g, base):
                for half in range(2):
                    src = bass.AP(x0_dram.tensor, base + (2 * LC * g + half) * PAIR,
                                  [[0, P // 2], [2 * PAIR, LC], [1, PAIR]])
                    sp.dma_start(x0_chunks(q, LC * g, LC)[64 * half:64 * half + 64, :, :],
                                 src).then_inc(bc_in[q][g], 16)

            def load_shared(pair):
                sp.wait_ge(p2_used, NL * (pair - 1) + 1)
                load_bc(pair % 2, NL - 1, pair * SLOT)

            def load_dense(col):
                sp.dma_start(dense_sb, dense_t[:, bass.ds(col, P)]).then_inc(dense_in, 16)

            def next_block(i):
                if i >= 1:
                    sp.wait_ge(h1_mm, i)
                load_dense(i * P)
                for q in range(2):
                    pair = 2 * i + q
                    if q == 0:
                        load_shared(pair + 1)
                        store_x0(q, (pair + 2) * SLOT, pair + 3)
                    load_rot(q, pair + 3, pair + 2)
                    if q == 1:
                        load_shared(pair + 1)
                    sp.wait_ge(x0_stored[q], 16 * (i + 2))
                    for g in range(NL - 1):
                        sp.wait_ge(p2_used, NL * pair + g + 2)
                        load_bc(q, g, (pair + 2) * SLOT)
                    if q == 0:
                        store_x0(1, (pair + 3) * SLOT, pair + 4)

            sp.dma_start(ids_sb[:], ids.rearrange("(t p) f -> p t f", p=P)).then_inc(ids_in, 16)
            sp.dma_start(ident[:], eye).then_inc(ident_in, 16)
            sp.dma_start(w0_sb[:], w0_fwd).then_inc(w0_in, 16)
            sp.dma_start(w0_bwd_sb, w0_bwd).then_inc(w0b_in, 16)
            sp.dma_start(w1_sb[:], w1.rearrange("(c a) h k -> (a h) c k", a=2)).then_inc(w1_in, 16)
            sp.dma_start(w2_sb[:], w2.rearrange("(c a) h k -> (a h) c k", a=2)).then_inc(w2_in, 16)
            for half in range(2):
                sp.dma_start(wt1_sb[64 * half:64 * half + 64, :, :],
                             w_top1[0:NZ * K, :].rearrange("(l k) n -> k l n", k=K)).then_inc(mlp_in, 16)
            sp.dma_start(wdense_sb, w_top1[NZ * K:NZ * K + ND, :]).then_inc(mlp_in, 16)
            sp.dma_start(wt2_sb[:], w_top2.rearrange("(c p) n -> p c n", p=P)).then_inc(mlp_in, 16)
            sp.dma_start(wt3_sb[:], w_top3).then_inc(mlp_in, 16)
            sp.dma_start(bt1_sb[:], b_top1).then_inc(mlp_in, 16)
            sp.dma_start(bt2_sb[:], b_top2).then_inc(mlp_in, 16)

            for q in range(2):
                store_x0(q, q * SLOT, q + 1)
                load_rot(q, q + 1, q or None)
                sp.wait_ge(x0_stored[q], 16)
                for g in range(NL - q):
                    load_bc(q, g, q * SLOT)
            for i in range(NB - 1):
                next_block(i)
            sp.wait_ge(h1_mm, NB - 1)
            load_dense((NB - 1) * P)
            load_shared(NP - 1)

        @block.gpsimd
        def _(pool):
            gathers = [(t, f) for t in range(NB) for f in range(M)]
            steps = [0]
            GATHERS = (4, 10, 6, 12)

            def gather(n):
                for t, f in gathers[:n]:
                    if f == 0 and t >= 1:
                        pool.wait_ge(transposed, 2 * t)
                    pool.indirect_dma_start(
                        out=gath[:, D * f:D * f + D], out_offset=None, in_=tables[f],
                        in_offset=bass.IndirectOffsetOnAxis(ap=ids_sb[:, t, f:f + 1], axis=0),
                    ).then_inc(gathered, 16)
                del gathers[:n]

            def add(out, a, b, then):
                nc.gpsimd.tensor_tensor(out, a, b, ALU.add).then_inc(then, 1)

            def sum_z(l, q, unit):
                r = relu_z[l]
                pool.wait_ge(acc_read, unit + 1)
                add(r[:, 0:256], r[:, 0:256], r[:, 256:512], z_step)
                steps[0] += 1
                pool.wait_ge(z_step, steps[0])
                if q == 0:
                    add(z[l][:], r[:, 0:128], r[:, 128:256], z_added[l])
                else:
                    add(r[:, 0:128], r[:, 0:128], r[:, 128:256], z_step)
                    steps[0] += 1
                    pool.wait_ge(z_step, steps[0])
                    add(z[l][:], z[l][:], r[:, 0:128], z_added[l])

            def half_chunk(pair):
                pool.wait_ge(x0rep_ready, pair + 1)
                pool.wait_ge(rot_in[1], 144 * (pair + 1))
                nc.gpsimd.tensor_tensor(rot[0:HALF, N0, :], x0rep[pair % 2][0:HALF, :], rot[0:HALF, N0, :],
                                        ALU.mult).then_inc(p0_pool, 1)

            def layer2(pair, g):
                pool.wait_ge(x2_sb_ready, pair + 1)
                pool.wait_ge(bc_in[pair % 2][g * GC // LC], 32 * (pair // 2 + 1))
                for c in range(GC * g, GC * g + GC):
                    chunk = x0_chunks(pair % 2, c, 1)[:, 0, :]
                    pool.wait_ge(p1_ready, NG * pair + g + 1)
                    nc.gpsimd.tensor_tensor(chunk, chunk, x2_sb[:], ALU.mult).then_inc(p2_pool, 1)

            pool.wait_ge(ids_in, 16)
            gather(M)
            gather(M)
            for p in range(NP):
                i, q = divmod(p, 2)
                if p >= 1:
                    sum_z(2, 1 - q, 3 * p)
                if 1 <= p < NP - 1 and q == 0:
                    half_chunk(p + 1)
                if q == 1:
                    sum_z(0, q, 3 * p - 1)
                    gather(GATHERS[1])
                    if 1 <= p < NP - 1:
                        half_chunk(p + 1)
                if p >= 2 and q == 0:
                    gather(GATHERS[3])
                if q == 1:
                    sum_z(1, q, 3 * p + 1)
                layer2(p, P2_POOL[0])
                if q == 0:
                    if i >= 1:
                        pool.wait_ge(h1_mm, i)
                    sum_z(0, q, 3 * p - 1 if p else 0)
                    sum_z(1, q, 3 * p + 1)
                layer2(p, P2_POOL[1])
                gather(GATHERS[0] if q == 0 else GATHERS[2])

        @block.scalar
        def _(act):
            def spread(bank, x_ps, ready):
                for t in range(2):
                    for half in range(2):
                        last = nc.scalar.activation(x_ps[64 * half:64 * half + 64, TILE * t:TILE * t + TILE],
                                                    bank[64 * t:64 * t + 64, :], ACT.Relu)
                last.then_inc(ready, 1)

            def spread_sb(bank, n):
                if not (isinstance(n, int) and n == 0):
                    act.wait_ge(p2_pool, GC * len(P2_POOL) * n)
                for t in range(2):
                    for half in range(2):
                        last = nc.scalar.activation(x2_sb[64 * half:64 * half + 64, TILE * t:TILE * t + TILE],
                                                    bank[64 * t:64 * t + 64, :], ACT.Relu)
                last.then_inc(x2_sb_ready, 1)

            def keep_z(bank, l):
                nc.scalar.activation(relu_z[l][:], bank[:], ACT.Relu).then_inc(acc_read, 1)

            def copy_x0(pair, q):
                act.wait_ge(transposed, pair + 1)
                for r, ready in enumerate((None, x0rows_ready, None, x0rep_ready)):
                    last = nc.scalar.activation(x0rep[q][M * r:M * r + M, :], aux[0:M, :], ACT.Copy)
                    if ready is not None:
                        last.then_inc(ready, 1)

            def finish_h1(block_, z1_added):
                act.wait_ge(h1_mm, block_ + 1)
                act.wait_ge(z_added[1], z1_added)
                for c in range(C1):
                    nc.scalar.activation(h1[:, c, :], aux[:, P * c:P * c + P], ACT.Relu,
                                         bias=bt1_sb[:, c:c + 1]).then_inc(h1_ready, 1)

            def finish_h2(block_, z2_added):
                act.wait_ge(h2_mm, block_ + 1)
                act.wait_ge(z_added[2], z2_added)
                for c in range(C2):
                    last = nc.scalar.activation(h2[:, c, :], aux[:, TILE + P * c:TILE + P * c + P], ACT.Relu,
                                                bias=bt2_sb[:, c:c + 1])
                last.then_inc(h2_ready, 1)

            def finish_y(block_):
                act.wait_ge(y_mm, block_ + 1)
                nc.scalar.activation(y_sb[:, bass.ds(block_, 1)], aux[:, TILE + 256:TILE + 257], ACT.Copy).then_inc(y_ready, 1)
                act.wait_ge(y_ready, block_ + 1)
                act.dma_start(y[bass.ds(block_ * P, P), :], y_sb[:, bass.ds(block_, 1)]).then_inc(y_out, 16)

            def two_pairs(i, first, last):
                for q in range(2):
                    p = 2 * i + q
                    bank, other = acc[(3 * q + 1) % 2], acc[(3 * q + 2) % 2]
                    act.wait_ge(p1_used, NG * (p + 1))
                    if not (first and q == 0):
                        act.wait_ge(p2_dve, P2_DVE * p)
                    spread(bank, x2_ps, x2_ready)
                    if not (first and q == 0):
                        act.wait_ge(z_added[1], p)
                    spread_sb(bank, p)
                    if q == 1 and not first:
                        act.wait_ge(h2_mm, i)
                    keep_z(bank, 1)
                    if q == 0 and not first:
                        finish_h1(i - 1, p + 1)
                    if q == 1 and not first:
                        finish_h2(i - 1, p)
                    if not (last and q == 1):
                        act.wait_ge(p0_used, p + 2)
                        act.wait_ge(p1_ready, NG * (p + 1))
                        spread(other, x1_ps, x1_ready)
                        act.wait_ge(z_added[0], p + 1)
                        keep_z(other, 0)
                    if q == 0 and not last:
                        for r in range(2):
                            act.wait_ge(p0_dve, p0_dve_done(p + r, 3 if first else 2))
                            if not first:
                                act.wait_ge(p0_pool, p + r - 1)
                            act.wait_ge(x0_stored[r], 16 * (i + 1))
                            copy_x0(p + 2 + r, r)
                    if last and q == 1:
                        bank = other
                    act.wait_ge(p2_used, NL * (p + 1))
                    if not (first and q == 0):
                        act.wait_ge(z_added[2], p)
                    if q == 1 and not first:
                        act.wait_ge(y_mm, i)
                    keep_z(bank, 2)
                    if q == 1 and not first:
                        finish_y(i - 1)

            copy_x0(0, 0)
            copy_x0(1, 1)
            act.wait_ge(p0_used, 1)
            spread(acc[0], x1_ps, x1_ready)
            keep_z(acc[0], 0)
            act.wait_ge(mlp_in, 7 * 16)
            two_pairs(0, True, False)
            with act.Fori(1, NB - 1) as i:
                two_pairs(i, False, False)
            two_pairs(NB - 1, False, True)
            finish_h1(NB - 1, NP)
            finish_h2(NB - 1, NP)
            finish_y(NB - 1)
            act.wait_ge(y_out, 16 * NB)

        @block.vector
        def _(dve):
            def layer0(pair, q, every):
                dve.wait_ge(x0rep_ready, pair + 1)
                xr = x0rep[q]
                for n in range(2):
                    chunks = rot[:, 2 * n:2 * n + 2, :]
                    dve.wait_ge(rot_in[n], (128, 144)[n] * (pair + 1))
                    nc.vector.tensor_tensor(chunks, xr[:].unsqueeze(1).broadcast_to([P, 2, PAIR]),
                                            chunks, ALU.mult).then_inc(p0_dve, 1)
                if every:
                    nc.vector.tensor_tensor(rot[0:HALF, N0, :], xr[0:HALF, :], rot[0:HALF, N0, :],
                                            ALU.mult).then_inc(p0_dve, 1)

            x1_bc = x1_ps[:].unsqueeze(1).broadcast_to([P, GC, PAIR])
            x2_bc = x2_ps[:].unsqueeze(1).broadcast_to([P, GC, PAIR])

            def two_pairs(i, first, last):
                for q in range(2):
                    p = 2 * i + q
                    dve.wait_ge(x1_ready, p + 1)
                    for g in range(NG):
                        if g % 2 == 0:
                            dve.wait_ge(bc_in[q][g * GC // LC], 32 * (i + 1))
                        if not (first and q == 0 and g < RING):
                            dve.wait_ge(p1_used, NG * p + g + 1 - RING)
                        nc.vector.tensor_tensor(ring[:, g % RING, :, :], x0_chunks(q, GC * g, GC), x1_bc,
                                                ALU.mult).then_inc(p1_ready, 1)
                    if not (last and q == 1):
                        layer0(p + 1, 1 - q, first and q == 0)
                    dve.wait_ge(x2_ready, p + 1)
                    for g in L2_ORDER:
                        if g in P2_POOL:
                            continue
                        chunk = x0_chunks(q, GC * g, GC)
                        nc.vector.tensor_tensor(chunk, chunk, x2_bc, ALU.mult).then_inc(p2_dve, 1)

            dve.wait_ge(w0_in, 16)
            dve.wait_ge(w0b_in, 16)
            for rows, cs in ((slice(M, 2 * M), slice(0, 1)), (slice(2 * M, P), slice(0, 1)), (slice(0, P), slice(1, N0)), (slice(0, HALF), slice(N0, N0 + 1))):
                last = nc.vector.tensor_tensor(w0_sb[rows, cs, :], w0_sb[rows, cs, :], w0_bwd_sb[rows, cs, :], ALU.add)
            last.then_inc(w0_sym, 1)
            dve.wait_ge(w0_sym, 1)
            layer0(0, 0, True)
            two_pairs(0, True, False)
            with dve.Fori(1, NB - 1) as i:
                two_pairs(i, False, False)
            two_pairs(NB - 1, False, True)
            r = relu_z[2]
            dve.wait_ge(acc_read, 3 * NP)
            nc.vector.tensor_tensor(r[:, 0:256], r[:, 0:256], r[:, 256:512], ALU.add).then_inc(z_last, 1)
            dve.wait_ge(z_last, 1)
            nc.vector.tensor_tensor(r[:, 0:128], r[:, 0:128], r[:, 128:256], ALU.add).then_inc(z_last, 1)
            dve.wait_ge(z_last, 2)
            dve.wait_ge(z_added[2], NP - 1)
            nc.vector.tensor_tensor(z[2][:], z[2][:], r[:, 0:128], ALU.add).then_inc(z_added[2], 1)

        @block.tensor
        def _(pe):
            def both(bank, w, prod, start, stop):
                for t in range(2):
                    last = nc.tensor.matmul(bank[64 * t:64 * t + 64, :], w, prod[:, TILE * t:TILE * t + TILE],
                                            start=start, stop=stop)
                return last

            def transpose_x0(q):
                g = gath[:].rearrange("p (m d) -> p m d", d=D)
                for dd in range(DP):
                    last = nc.tensor.transpose(aux[0:M, P * dd:P * dd + P], g[:, :, DP * q + dd], ident[:])
                last.then_inc(transposed, 1)

            def layer0(pair, bank, every):
                for c in range(N0):
                    if c % 2 == 0:
                        pe.wait_ge(p0_dve, p0_dve_done(pair, c // 2 + 1))
                    both(bank, w0_sb[:, c, :], rot[:, c, :], c == 0, False)
                if every:
                    pe.wait_ge(p0_dve, p0_dve_done(pair, 3))
                else:
                    pe.wait_ge(p0_pool, pair - 1)
                both(bank, w0_sb[0:HALF, N0, :], rot[0:HALF, N0, :], False, True).then_inc(p0_used, 1)

            def mlp_h1(block_):
                for l in range(NZ):
                    if l == NZ - 1:
                        pe.wait_ge(dense_in, 16 * (block_ + 1))
                        for c in range(C1):
                            nc.tensor.matmul(aux[:, P * c:P * c + P], wdense_sb[:, P * c:P * c + P], dense_sb,
                                             start=False, stop=False, skip_group_check=True)
                    pe.wait_ge(z_added[l], 2 * (block_ + 1))
                    for c in range(C1):
                        last = nc.tensor.matmul(aux[:, P * c:P * c + P], wt1_sb[:, l, P * c:P * c + P], z[l][:],
                                                start=(l == 0 and c == 0), stop=(l == NZ - 1), skip_group_check=True)
                last.then_inc(h1_mm, 1)

            def mlp_h2(block_):
                for c in range(C1):
                    pe.wait_ge(h1_ready, C1 * block_ + c + 1)
                    for n in range(C2):
                        last = nc.tensor.matmul(aux[:, TILE + P * n:TILE + P * n + P], wt2_sb[:, c, P * n:P * n + P],
                                                h1[:, c, :], start=(c == 0 and n == 0), stop=(c == C1 - 1),
                                                skip_group_check=True)
                last.then_inc(h2_mm, 1)

            def mlp_y(block_):
                pe.wait_ge(h2_ready, block_ + 1)
                for c in range(C2):
                    last = nc.tensor.matmul(aux[:, TILE + 256:TILE + 257], h2[:, c, :], wt3_sb[:, c:c + 1],
                                            start=(c == 0), stop=(c == C2 - 1))
                last.then_inc(y_mm, 1)

            def two_pairs(i, first, last):
                for q in range(2):
                    p = 2 * i + q
                    bank, other = acc[(3 * q + 1) % 2], acc[(3 * q + 2) % 2]
                    if not (first and q == 0):
                        pe.wait_ge(acc_read, 3 * p)
                    for g in range(NG):
                        pe.wait_ge(p1_ready, NG * p + g + 1)
                        for c in range(GC):
                            done = both(bank, w1_sb[:, GC * g + c, :], ring[:, g % RING, c, :],
                                        g == 0 and c == 0, g == NG - 1 and c == GC - 1)
                        done.then_inc(p1_used, 1)
                    if q == 0 and not first:
                        pe.wait_ge(x0rep_ready, 2 * i + 2)
                        mlp_h1(i - 1)
                    if q == 1 and not first:
                        if not last:
                            pe.wait_ge(x0rep_ready, 2 * i + 4)
                        mlp_h2(i - 1)
                    if not (last and q == 1):
                        pe.wait_ge(acc_read, 3 * p + 1)
                        layer0(p + 1, other, first and q == 0)
                    if last and q == 1:
                        bank = other
                    pe.wait_ge(acc_read, 3 * p + 2 - (1 if last and q == 1 else 0))
                    for n, g in enumerate(L2_ORDER):
                        if n == T_AT[0] and q == 0 and not last:
                            pe.wait_ge(gathered, 16 * M * (i + 2))
                            if not first:
                                pe.wait_ge(h1_ready, C1 * i)
                            transpose_x0(0)
                        if n == T_AT[1] and q == 0 and not last:
                            pe.wait_ge(x0rep_ready, 2 * i + 3)
                            transpose_x0(1)
                        if g in P2_POOL:
                            pe.wait_ge(p2_pool, GC * (len(P2_POOL) * p + P2_POOL.index(g) + 1))
                        else:
                            pe.wait_ge(p2_dve, P2_DVE * p + [k for k in L2_ORDER if k not in P2_POOL].index(g) + 1)
                        for c in range(GC):
                            done = both(bank, w2_sb[:, GC * g + c, :], x0_chunks(q, GC * g + c, 1)[:, 0, :],
                                        n == 0 and c == 0, n == NG - 1 and c == GC - 1)
                        if (n + 1) * GC % LC == 0:
                            done.then_inc(p2_used, 1)
                    if q == 1 and not first:
                        mlp_y(i - 1)

            pe.wait_ge(ident_in, 16)
            pe.wait_ge(gathered, 16 * M)
            transpose_x0(0)
            pe.wait_ge(x0rep_ready, 1)
            transpose_x0(1)
            pe.wait_ge(w0_sym, 1)
            layer0(0, acc[0], True)
            pe.wait_ge(w1_in, 16)
            pe.wait_ge(w2_in, 16)
            pe.wait_ge(mlp_in, 7 * 16)
            two_pairs(0, True, False)
            with pe.Fori(1, NB - 1) as i:
                two_pairs(i, False, False)
            two_pairs(NB - 1, False, True)
            mlp_h1(NB - 1)
            mlp_h2(NB - 1)
            mlp_y(NB - 1)


def layer0_rows():
    part, chunk = np.meshgrid(np.arange(P), np.arange(N0 + 1), indexing="ij")
    m = part % M
    j = 4 * chunk + part // M
    h = (m + j) % M
    return M * m + h, M * h + m


def kernel(**inputs):
    import concourse.bacc as bacc
    from concourse.bass_utils import run_bass_kernel_spmd

    fwd, bwd = layer0_rows()
    w0 = np.asarray(inputs["L0_rec_W0"]).reshape(M * M, K)
    arrays = {
        "dense_t": np.ascontiguousarray(np.asarray(inputs["dense_ctx"]).T),
        "ids": np.ascontiguousarray(inputs["ids"]),
        "w0_fwd": np.ascontiguousarray(w0[fwd]),
        "w0_bwd": np.ascontiguousarray(w0[bwd]),
        "w1": np.ascontiguousarray(inputs["L0_rec_W1"]),
        "w2": np.ascontiguousarray(inputs["L0_rec_W2"]),
        "w_top1": np.ascontiguousarray(inputs["W_top1"]),
        "b_top1": np.ascontiguousarray(np.asarray(inputs["b_top1"]).reshape(-1, P).T),
        "w_top2": np.ascontiguousarray(inputs["W_top2"]),
        "b_top2": np.ascontiguousarray(np.asarray(inputs["b_top2"]).reshape(-1, P).T),
        "w_top3": np.ascontiguousarray(np.asarray(inputs["W_top3"]).reshape(-1, P).T),
        "eye": np.eye(P, dtype=np.float32),
    }
    for f in range(M):
        arrays[f"tbl_{f}"] = np.ascontiguousarray(inputs[f"tbl_{f}"])

    nc = bacc.Bacc("TRN2", target_bir_lowering=False, num_devices=1)
    ap = {n: nc.dram_tensor(n, a.shape, mybir.dt.from_np(a.dtype), kind="ExternalInput").ap()
          for n, a in arrays.items()}
    y = nc.dram_tensor("y", (arrays["ids"].shape[0], 1), F32, kind="ExternalOutput").ap()
    build(nc, ap["dense_t"], ap["ids"], [ap[f"tbl_{f}"] for f in range(M)], ap["w0_fwd"], ap["w0_bwd"],
          ap["w1"], ap["w2"], ap["w_top1"], ap["b_top1"], ap["w_top2"], ap["b_top2"], ap["w_top3"],
          ap["eye"], y)
    r = run_bass_kernel_spmd(nc, [arrays], core_ids=[0])
    return r.results[0]["y"]
```

```python
from contextlib import ExitStack

import numpy as np
import concourse.bass as bass
from concourse import mybir

F32 = mybir.dt.float32
I32 = mybir.dt.int32
ALU = mybir.AluOpType
ACT = mybir.ActivationFunctionType

P = 128
M = 32
D = 16
K = 64
TILE = 512
PAIR = 2 * TILE
DP = PAIR // P
NC = M * K // P
GC = 2
NG = NC // GC
LC = 4
NL = NC // LC
RING = 4
L2_ORDER = [*range(NG - LC // GC, NG), *range(NG - LC // GC)]
N0 = M // 8
HALF = M // 2
ROWS = M + HALF
LP = 125
LOOKUPS = 11
LP_MAX = 10
ONE_HOTS = 3
LQ = 4
H1 = 512
H2 = 256


def looked_up_fields(rows):
    return sorted(sorted(range(M), key=lambda f: rows[f])[:LOOKUPS])


def build(nc, fold, ids_first, small_tables, row_no, dense_t, ids, tables, w0_fwd, w0_bwd, w1, w2,
          w_top1, b_top1, w_top2, b_top2, w_top3, eye, y):
    B = ids.shape[0]
    NB = B // P
    NP = 2 * NB
    ND = dense_t.shape[0]
    C1 = H1 // P
    C2 = H2 // P
    NZ = 3
    table_rows = [t.shape[0] for t in tables]
    looked = looked_up_fields(table_rows)
    gathers = [(0, f) for f in range(M) if f not in looked] + [(t, f) for t in range(1, NB) for f in range(M)]

    x0_dram = nc.dram_tensor("x0_scratch", (NP, ROWS, PAIR), F32, kind="Internal").ap()

    with ExitStack() as ctx:
        def sb(name, shape, dt=F32):
            return ctx.enter_context(nc.sbuf_tensor(name, shape, dt))

        def psum(name, shape):
            return ctx.enter_context(nc.psum_tensor(name, shape, F32))

        def sem(name):
            return ctx.enter_context(nc.semaphore(name))

        ids_sb = sb("ids_sb", [P, NB, M], I32)
        gath = sb("gath", [P, M * D])
        ident = sb("ident", [P, P])
        x0rep = [sb(f"x0rep{q}", [P, PAIR]) for q in range(2)]
        rot = sb("rot", [P, N0 + 1, PAIR])
        x0bc_own = [sb(f"x0bc_own{q}", [P, NC - LC, PAIR]) for q in range(2)]
        x0bc_shared = sb("x0bc_shared", [P, LC, PAIR])
        x2_sb = sb("x2_sb", [P, PAIR])
        ring = sb("ring", [P, RING, GC, PAIR])
        w0_sb = sb("w0_sb", [P, N0 + 1, K])
        w1_sb = sb("w1_sb", [P, NC, K])
        w2_sb = sb("w2_sb", [P, NC, K])
        wt1_sb = sb("wt1_sb", [P, 2, H1])
        fold_sb = sb("fold_sb", [P, K])
        wt2_sb = sb("wt2_sb", [P, C1, H2])
        wt3_sb = sb("wt3_sb", [P, C2])
        bt1_sb = sb("bt1_sb", [P, C1])
        bt2_sb = sb("bt2_sb", [P, C2])
        relu_z = [sb(f"relu_z{l}", [P, TILE]) for l in range(NZ)]
        z = [sb(f"z{l}", [P, P]) for l in range(NZ)]
        mlp_in_01 = sb("mlp_in_01", [2 * K, P])
        mlp_in_2d = sb("mlp_in_2d", [K + ND, P])
        h1 = relu_z[1][:].rearrange("p (c n) -> p c n", n=P)
        h2 = relu_z[2][:, 0:C2 * P].rearrange("p (c n) -> p c n", n=P)
        y_sb = sb("y_sb", [P, NB])
        gath_first = x0bc_own[1][:, 0, 0:M * D]
        fields_rep = x0bc_own[1][:, 1, :].rearrange("p (r d) -> p r d", d=DP)
        fields_round = x0bc_own[1][:, 2:4, :].rearrange("p c n -> p (c n)")[:, 0:5 * M * DP].rearrange(
            "p (a m d) -> p a m d", m=M, d=DP)
        ids_bc = x0bc_own[1][0:LP, 4:6, :].rearrange("p c n -> p (c n)")[:, 0:len(looked) * P].bitcast(I32)
        small_sb = x0bc_own[1][0:LP, 6:8, :].rearrange("p c n -> p (c n)")[:, 0:small_tables.shape[1]]
        lookup_sb = [x0bc_own[1][:, 11, P * n:P * n + P] for n in range(2)]
        row_no_sb = x0bc_own[1][0:LP, 8, 0:row_no.shape[1]].bitcast(I32)
        spread_fields = [x0bc_own[1][:, n, :].rearrange("p (a r d) -> p a r d", a=2, d=DP) for n in (9, 10, 4, 5)]
        one_hot = [ring[0:LP, 1 + n, :, :].rearrange("p c n -> p (c n)")[:, 0:LP_MAX * P].rearrange(
            "p (n s) -> p n s", s=P) for n in range(ONE_HOTS)]
        w0_bwd_sb = ring[:, 0, 0, 0:(N0 + 1) * K].rearrange("p (c k) -> p c k", k=K)

        acc = [psum(f"acc{n}", [P, TILE]) for n in range(2)]
        x1_ps = psum("x1_ps", [P, PAIR])
        x2_ps = psum("x2_ps", [P, PAIR])
        aux = psum("aux", [P, PAIR])

        lookup_ps = [x1_ps[:, 0:P], x1_ps[:, TILE:TILE + P], x2_ps[:, 0:P]]
        lookup_t_ps = [x2_ps[:, TILE:TILE + P], acc[1][:, 0:P]]

        ids_in = sem("ids_in")
        ident_in = sem("ident_in")
        w0_in = sem("w0_in")
        w0b_in = sem("w0b_in")
        w1_in = sem("w1_in")
        w2_in = sem("w2_in")
        mlp_in = sem("mlp_in")
        dense_in = sem("dense_in")
        w0_sym = sem("w0_sym")
        first_gathered = [sem(f"first_gathered{g}") for g in range(NL)]
        gathered = sem("gathered")
        ids_first_in = sem("ids_first_in")
        row_no_in = sem("row_no_in")
        small_in = sem("small_in")
        chunk_spread = sem("chunk_spread")
        one_hot_ready = sem("one_hot_ready")
        lookup_mm = sem("lookup_mm")
        lookup_copied = sem("lookup_copied")
        lookup_t = sem("lookup_t")
        looked_up = sem("looked_up")
        transposed = sem("transposed")
        x0rep_ready = sem("x0rep_ready")
        x0_stored = [sem(f"x0_stored{q}") for q in range(2)]
        rows_placed = sem("rows_placed")
        chunk_placed = sem("chunk_placed")
        chunk_copied = sem("chunk_copied")
        rep_ordered = sem("rep_ordered")
        round_ordered = sem("round_ordered")
        rep_in = [sem(f"rep_in{q}") for q in range(2)]
        rot_in = [sem(f"rot_in{n}") for n in range(2)]
        bc_in = [[sem(f"bc_in{q}_{g}") for g in range(NL)] for q in range(2)]
        p0_dve = sem("p0_dve")
        p0_pool = sem("p0_pool")
        p1_ready = sem("p1_ready")
        p2_dve = sem("p2_dve")
        p2_pool = sem("p2_pool")
        p0_used = sem("p0_used")
        p1_used = sem("p1_used")
        p2_used = sem("p2_used")
        x1_ready = sem("x1_ready")
        x1_b_ready = sem("x1_b_ready")
        x2_ready = sem("x2_ready")
        x2_sb_ready = sem("x2_sb_ready")
        acc_read = sem("acc_read")
        z_step = sem("z_step")
        z_last = sem("z_last")
        z_added = [sem(f"z_added{l}") for l in range(NZ)]
        z_folded = sem("z_folded")
        mlp_in_ready = sem("mlp_in_ready")
        h1_mm = sem("h1_mm")
        h1_ready = sem("h1_ready")
        h2_mm = sem("h2_mm")
        h2_ready = sem("h2_ready")
        y_mm = sem("y_mm")
        y_ready = sem("y_ready")
        y_out = sem("y_out")

        def fold_col(block_):
            return TILE if isinstance(block_, int) and block_ == NB - 1 else P

        P2_POOL = (1, 4)
        T_AT = (5, 7)
        FOLD_AT = (3, 6)
        P2_DVE = NG - len(P2_POOL)
        DEFERRED = 1

        def p0_dve_done(pair, n):
            if isinstance(pair, int) and pair < 2:
                return 5 * pair + n
            return 2 * pair + 4 + n

        LOAD = M // NL
        LOOK_AHEAD = 6

        def wait_first_fields(engine, g, lookups=True):
            engine.wait_ge(first_gathered[g], 16 * sum(f // LOAD == g for t, f in gathers if t == 0))
            if lookups:
                engine.wait_ge(looked_up, sum(f // LOAD <= g for f in looked))

        FIRST_ROWS = [(P, x2_ps), (P, x1_ps), (P, aux), (P, x2_ps), (HALF, x1_ps)]
        WARM_UP = 16
        PLACED = 2
        BY_LOOKUPS = LC
        BY_LAYER0 = LC + 1

        def spread_place(c):
            return spread_fields[(0, 1, 0, 1, 0, 3, 2, 1)[c]]

        def bc_loaded(q, g, i):
            return 32 * i if q == 0 and g < PLACED else 32 * (i + 1)

        def x0_chunks(q, c, n):
            if c < NC - LC:
                return x0bc_own[q][:, c:c + n, :]
            return x0bc_shared[:, c - (NC - LC):c - (NC - LC) + n, :]

        block = ctx.enter_context(nc.Block())

        @block.sync
        def _(sp):
            SLOT = ROWS * PAIR

            def store_x0(q, base):
                for row, rows in ((0, M), (M, HALF)):
                    dst = bass.AP(x0_dram.tensor, base + row * PAIR, [[PAIR, rows], [1, PAIR]])
                    sp.dma_start(dst, x0rep[q][0:rows, :]).then_inc(x0_stored[q], 16)

            def load_rot(q, pair):
                base = pair * SLOT
                src = bass.AP(x0_dram.tensor, base + PAIR, [[PAIR, 3], [PAIR, M], [1, PAIR]])
                sp.dma_start(x0rep[q][M:P, :], src).then_inc(rep_in[q], 16)
                sp.wait_ge(p0_used, pair)
                for c in range(N0):
                    src = bass.AP(x0_dram.tensor, base + (4 * c + 3) * PAIR, [[0, 4], [PAIR, M], [1, PAIR]])
                    sp.dma_start(rot[:, c, :], src).then_inc(rot_in[c // 2], 16)
                src = bass.AP(x0_dram.tensor, base + HALF * PAIR, [[PAIR, HALF], [1, PAIR]])
                sp.dma_start(rot[0:HALF, N0, :], src).then_inc(rot_in[1], 16)

            def load_bc(q, g, base):
                for half in range(2):
                    src = bass.AP(x0_dram.tensor, base + (2 * LC * g + half) * PAIR,
                                  [[0, P // 2], [2 * PAIR, LC], [1, PAIR]])
                    sp.dma_start(x0_chunks(q, LC * g, LC)[64 * half:64 * half + 64, :, :],
                                 src).then_inc(bc_in[q][g], 16)

            def load_shared(pair):
                sp.wait_ge(p2_used, NL * (pair - 1) + 1)
                load_bc(pair % 2, NL - 1, pair * SLOT)

            def load_dense(col):
                sp.dma_start(mlp_in_2d[K:K + ND, :], dense_t[:, bass.ds(col, P)]).then_inc(dense_in, 16)

            def next_block(i):
                if i >= 1:
                    sp.wait_ge(h1_mm, i)
                load_dense(i * P)
                for q in range(2):
                    pair = 2 * i + q
                    if q == 0:
                        load_shared(pair + 1)
                        sp.wait_ge(x0rep_ready, pair + 3)
                        store_x0(0, (pair + 2) * SLOT)
                    else:
                        load_shared(pair + 1)
                    sp.wait_ge(x0_stored[q], 32 * (i + 2))
                    load_rot(q, pair + 2)
                    for g in range(NL - 1):
                        sp.wait_ge(p2_used, NL * pair + g + 2)
                        load_bc(q, g, (pair + 2) * SLOT)
                    if q == 0:
                        sp.wait_ge(x0rep_ready, pair + 4)
                        store_x0(1, (pair + 3) * SLOT)

            sp.dma_start(ids_sb[:], ids.rearrange("(t p) f -> p t f", p=P)).then_inc(ids_in, 16)
            sp.dma_start(ident[:], eye).then_inc(ident_in, 16)
            sp.dma_start(row_no_sb, row_no).then_inc(row_no_in, 16)
            sp.dma_start(ids_bc, bass.AP(ids_first.tensor, 0, [[0, LP], [1, len(looked) * P]])).then_inc(ids_first_in, 16)
            sp.dma_start(small_sb, small_tables).then_inc(small_in, 16)
            sp.dma_start(w0_sb[:], w0_fwd).then_inc(w0_in, 16)
            sp.dma_start(w0_bwd_sb, w0_bwd).then_inc(w0b_in, 16)
            wait_first_fields(sp, 0, lookups=False)
            sp.dma_start(w1_sb[:], w1.rearrange("(c a) h k -> (a h) c k", a=2)).then_inc(w1_in, 16)
            sp.dma_start(w2_sb[:], w2.rearrange("(c a) h k -> (a h) c k", a=2)).then_inc(w2_in, 16)
            sp.dma_start(wt1_sb[:, 0, :], w_top1[0:2 * K, :]).then_inc(mlp_in, 16)
            sp.dma_start(wt1_sb[0:K + ND, 1, :], w_top1[2 * K:NZ * K + ND, :]).then_inc(mlp_in, 16)
            sp.dma_start(fold_sb[:], fold).then_inc(mlp_in, 16)
            sp.dma_start(wt2_sb[:], w_top2.rearrange("(c p) n -> p c n", p=P)).then_inc(mlp_in, 16)
            sp.dma_start(wt3_sb[:], w_top3).then_inc(mlp_in, 16)
            sp.dma_start(bt1_sb[:], b_top1).then_inc(mlp_in, 16)
            sp.dma_start(bt2_sb[:], b_top2).then_inc(mlp_in, 16)

            sp.wait_ge(x0rep_ready, 1)
            store_x0(0, 0)
            sp.wait_ge(x0_stored[0], 32)
            for g in range(PLACED, NL - 1):
                load_bc(0, g, 0)
            sp.wait_ge(x0rep_ready, 2)
            store_x0(1, SLOT)
            load_bc(0, NL - 1, 0)
            sp.wait_ge(x0_stored[1], 32)
            load_rot(1, 1)
            sp.wait_ge(gathered, 16 * M)
            sp.wait_ge(chunk_placed, 2 * LC * PLACED)
            for g in range(NL - 1):
                load_bc(1, g, SLOT)
            for i in range(NB - 1):
                next_block(i)
            sp.wait_ge(h1_mm, NB - 1)
            load_dense((NB - 1) * P)
            load_shared(NP - 1)

        @block.gpsimd
        def _(pool):
            ahead = list(gathers)
            steps = [0]
            GATHERS = (4, 10, 6, 12)

            def gather(n):
                for t, f in ahead[:n]:
                    if t >= 2 and f == 0:
                        pool.wait_ge(transposed, 2 * t - 1)
                    pool.indirect_dma_start(
                        out=(gath if t else gath_first)[:, D * f:D * f + D], out_offset=None, in_=tables[f],
                        in_offset=bass.IndirectOffsetOnAxis(ap=ids_sb[:, t, f:f + 1], axis=0),
                    ).then_inc(gathered if t else first_gathered[f // LOAD], 16)
                del ahead[:n]

            def add(out, a, b, then):
                nc.gpsimd.tensor_tensor(out, a, b, ALU.add).then_inc(then, 1)

            def sum_z(l, q, unit):
                r = relu_z[l]
                pool.wait_ge(acc_read, unit + 1)
                add(r[:, 0:256], r[:, 0:256], r[:, 256:512], z_step)
                steps[0] += 1
                pool.wait_ge(z_step, steps[0])
                if q == 0:
                    add(z[l][:], r[:, 0:128], r[:, 128:256], z_added[l])
                else:
                    add(r[:, 0:128], r[:, 0:128], r[:, 128:256], z_step)
                    steps[0] += 1
                    pool.wait_ge(z_step, steps[0])
                    add(z[l][:], z[l][:], r[:, 0:128], z_added[l])

            def half_chunk(pair):
                pool.wait_ge(x0rep_ready, pair + 1)
                pool.wait_ge(rot_in[1], 48 * pair)
                nc.gpsimd.tensor_tensor(rot[0:HALF, N0, :], x0rep[pair % 2][0:HALF, :], rot[0:HALF, N0, :],
                                        ALU.mult).then_inc(p0_pool, 1)

            def layer2(pair, g):
                pool.wait_ge(x2_sb_ready, pair + 1)
                if pair or g * GC // LC >= PLACED:
                    pool.wait_ge(bc_in[pair % 2][g * GC // LC], bc_loaded(pair % 2, g * GC // LC, pair // 2))
                for c in range(GC * g, GC * g + GC):
                    chunk = x0_chunks(pair % 2, c, 1)[:, 0, :]
                    pool.wait_ge(p1_ready, NG * pair + g + 1)
                    nc.gpsimd.tensor_tensor(chunk, chunk, x2_sb[:], ALU.mult).then_inc(p2_pool, 1)

            pool.wait_ge(ids_in, 16)
            gather(M - len(looked))
            gather(M)
            for p in range(NP):
                i, q = divmod(p, 2)
                if p == NP - 1:
                    sum_z(0, 1, 3 * p - 1)
                    layer2(p, P2_POOL[0])
                    sum_z(1, 1, 3 * p)
                    sum_z(2, 0, 3 * p + 1)
                    layer2(p, P2_POOL[1])
                    break
                if p >= 1:
                    sum_z(2, 1 - q, 3 * p)
                if q == 1:
                    sum_z(0, q, 3 * p - 1)
                    gather(GATHERS[1])
                    if p >= 1:
                        half_chunk(p + 1)
                if p >= 2 and q == 0:
                    gather(GATHERS[3])
                    half_chunk(p + 1)
                if q == 1:
                    sum_z(1, q, 3 * p + 1)
                layer2(p, P2_POOL[0])
                if q == 0:
                    if i >= 1:
                        pool.wait_ge(z_folded, 2 * i)
                    sum_z(0, q, 3 * p - 1 if p else 0)
                    sum_z(1, q, 3 * p + 1)
                layer2(p, P2_POOL[1])
                gather(GATHERS[0] if q == 0 else GATHERS[2])

        @block.scalar
        def _(act):
            def spread(bank, x_ps, ready, tiles=2):
                for t in range(tiles):
                    for half in range(2):
                        last = nc.scalar.activation(x_ps[64 * half:64 * half + 64, TILE * t:TILE * t + TILE],
                                                    bank[64 * t:64 * t + 64, :], ACT.Relu)
                last.then_inc(ready, 1)

            def spread_sb(bank, n):
                if not (isinstance(n, int) and n == 0):
                    act.wait_ge(p2_pool, GC * len(P2_POOL) * n)
                for t in range(2):
                    for half in range(2):
                        last = nc.scalar.activation(x2_sb[64 * half:64 * half + 64, TILE * t:TILE * t + TILE],
                                                    bank[64 * t:64 * t + 64, :], ACT.Relu)
                last.then_inc(x2_sb_ready, 1)

            def keep_z(bank, l):
                nc.scalar.activation(relu_z[l][:], bank[:], ACT.Relu).then_inc(acc_read, 1)

            def copy_x0(pair, q):
                act.wait_ge(transposed, pair)
                nc.scalar.activation(x0rep[q][0:M, :], aux[0:M, :], ACT.Copy).then_inc(x0rep_ready, 1)

            def copy_z01(block_):
                act.wait_ge(z_folded, 2 * block_ + 1)
                nc.scalar.activation(mlp_in_01[:], aux[:, 0:P], ACT.Copy).then_inc(mlp_in_ready, 1)

            def copy_z2(block_):
                act.wait_ge(z_folded, 2 * block_ + 2)
                col = fold_col(block_)
                nc.scalar.activation(mlp_in_2d[0:K, :], aux[0:K, col:col + P], ACT.Copy).then_inc(mlp_in_ready, 1)

            def finish_h1(block_, z1_added):
                act.wait_ge(h1_mm, block_ + 1)
                act.wait_ge(z_added[1], z1_added)
                for c in range(C1):
                    nc.scalar.activation(h1[:, c, :], aux[:, P * c:P * c + P], ACT.Relu,
                                         bias=bt1_sb[:, c:c + 1]).then_inc(h1_ready, 1)

            def finish_h2(block_, z2_added):
                act.wait_ge(h2_mm, block_ + 1)
                act.wait_ge(z_added[2], z2_added)
                for c in range(C2):
                    last = nc.scalar.activation(h2[:, c, :], aux[:, TILE + P * c:TILE + P * c + P], ACT.Relu,
                                                bias=bt2_sb[:, c:c + 1])
                last.then_inc(h2_ready, 1)

            def finish_y(block_):
                act.wait_ge(y_mm, block_ + 1)
                nc.scalar.activation(y_sb[:, bass.ds(block_, 1)], aux[:, TILE + 256:TILE + 257],
                                     ACT.Copy).then_inc(y_ready, 1)
                act.wait_ge(y_ready, block_ + 1)
                act.dma_start(y[bass.ds(block_ * P, P), :], y_sb[:, bass.ds(block_, 1)]).then_inc(y_out, 16)

            def two_pairs(i, first, last):
                for q in range(2):
                    p = 2 * i + q
                    bank, other = acc[(3 * q + 1) % 2], acc[(3 * q + 2) % 2]
                    if q == 0 and not first:
                        copy_z01(i - 1)
                        copy_z2(i - 1)
                    act.wait_ge(p1_used, NG * (p + 1))
                    if not (first and q == 0):
                        act.wait_ge(p2_dve, P2_DVE * p)
                    spread(bank, x2_ps, x2_ready)
                    if not (first and q == 0):
                        act.wait_ge(z_added[1], p)
                    spread_sb(bank, p)
                    if q == 1 and not first:
                        act.wait_ge(h2_mm, i)
                    keep_z(bank, 1)
                    if q == 0 and not first:
                        finish_h1(i - 1, p + 1)
                    if last and q == 1:
                        act.wait_ge(p2_used, NL * p)
                        act.wait_ge(z_added[2], p - 1)
                        keep_z(acc[1], 2)
                    if q == 1 and not first:
                        finish_h2(i - 1, p)
                    if not (last and q == 1):
                        act.wait_ge(p0_used, p + 2)
                        act.wait_ge(p1_ready, NG * (p + 1))
                        spread(other, x1_ps, x1_ready)
                        act.wait_ge(z_added[0], p + 1)
                        keep_z(other, 0)
                    if q == 0 and not last:
                        for r in range(2):
                            act.wait_ge(p0_dve, p0_dve_done(p + r, (5, 3)[r] if first else 2))
                            if not first:
                                act.wait_ge(p0_pool, p + r - 1)
                            act.wait_ge(x0_stored[r], 32 * (i + 1))
                            copy_x0(p + 2 + r, r)
                    if last and q == 0:
                        continue
                    if last:
                        copy_z01(i)
                        bank = x1_ps[:, 0:TILE]
                    act.wait_ge(p2_used, NL * (p + 1))
                    if not (first and q == 0):
                        act.wait_ge(z_added[2], p)
                    if q == 1 and not first:
                        act.wait_ge(y_mm, i)
                    keep_z(bank, 2)
                    if q == 1 and not first:
                        finish_y(i - 1)

            def order_round(g, loads):
                f = slice(LOAD * g, LOAD * (g + loads))
                src = gath_first.rearrange("p (m d) -> p m d", d=D)[:, f, 0:DP].unsqueeze(1)
                return nc.scalar.activation(fields_round[:, :, f, :],
                                            src.broadcast_to([P, 5, LOAD * loads, DP]), ACT.Copy)

            def copy_chunk(c):
                for t in range(2):
                    act.wait_ge(chunk_placed, 2 * c + t + 1)
                    nc.scalar.activation(x0_chunks(0, c, 1)[:, 0, TILE * t:TILE * t + TILE],
                                         aux[:, TILE * t:TILE * t + TILE], ACT.Copy).then_inc(chunk_copied, 1)

            for k, f in enumerate(looked):
                c = k - LOOK_AHEAD
                if 0 <= c < BY_LOOKUPS:
                    copy_chunk(c)
                if (k + 1) % LQ and k + 1 < len(looked):
                    continue
                j, n = k // LQ, k % LQ + 1
                act.wait_ge(lookup_mm, k + 1)
                if j >= 2:
                    act.wait_ge(lookup_t, j - 1)
                nc.scalar.activation(lookup_sb[j % 2][0:32 * n, :], lookup_ps[j % 3][0:32 * n, :],
                                     ACT.Copy).then_inc(lookup_copied, 1)
                act.wait_ge(lookup_t, j + 1)
                for m in range(n):
                    g = looked[LQ * j + m]
                    nc.scalar.activation(gath_first[:, D * g:D * g + D], lookup_t_ps[j % 2][:, 32 * m:32 * m + D],
                                         ACT.Copy).then_inc(looked_up, 1)
            copy_chunk(BY_LOOKUPS)
            act.wait_ge(looked_up, len(looked))
            for g in range(NL - 1):
                wait_first_fields(act, g, lookups=False)
            order_round(0, NL - 1)
            for c in range(BY_LOOKUPS + 1, BY_LAYER0):
                copy_chunk(c)
            wait_first_fields(act, NL - 1, lookups=False)
            order_round(NL - 1, 1).then_inc(round_ordered, 1)
            act.wait_ge(rows_placed, 1)
            nc.scalar.activation(x0rep[0][:], aux[:], ACT.Copy).then_inc(x0rep_ready, 1)
            act.wait_ge(p0_used, 1)
            act.wait_ge(p0_dve, p0_dve_done(0, 5))
            spread(acc[0], x1_ps, x1_ready, 1)
            copy_x0(1, 1)
            for c in range(BY_LAYER0, LC * PLACED):
                copy_chunk(c)
            act.wait_ge(x1_b_ready, 1)
            keep_z(acc[0], 0)
            act.wait_ge(mlp_in, 7 * 16)
            two_pairs(0, True, False)
            with act.Fori(1, NB - 1) as i:
                two_pairs(i, False, False)
            two_pairs(NB - 1, False, True)
            copy_z2(NB - 1)
            finish_h1(NB - 1, NP)
            finish_h2(NB - 1, NP)
            finish_y(NB - 1)
            act.wait_ge(y_out, 16 * NB)

        @block.vector
        def _(dve):
            def layer0(pair, q, reps, every):
                dve.wait_ge(x0rep_ready, pair + 1)
                dve.wait_ge(rep_in[q], 16 * reps)
                xr = x0rep[q]
                for n in range(2):
                    chunks = rot[:, 2 * n:2 * n + 2, :]
                    dve.wait_ge(rot_in[n], (32, 48)[n] * pair)
                    nc.vector.tensor_tensor(chunks, xr[:].unsqueeze(1).broadcast_to([P, 2, PAIR]),
                                            chunks, ALU.mult).then_inc(p0_dve, 1)
                if every:
                    nc.vector.tensor_tensor(rot[0:HALF, N0, :], xr[0:HALF, :], rot[0:HALF, N0, :],
                                            ALU.mult).then_inc(p0_dve, 1)

            x1_bc = x1_ps[:].unsqueeze(1).broadcast_to([P, GC, PAIR])
            x2_bc = x2_ps[:].unsqueeze(1).broadcast_to([P, GC, PAIR])

            def two_pairs(i, first, last):
                for q in range(2):
                    p = 2 * i + q
                    dve.wait_ge(x1_ready, p + 1)
                    for g in range(NG):
                        load = g * GC // LC
                        if first and q == 0 and load < PLACED:
                            dve.wait_ge(chunk_copied, 2 * GC * (g + 1))
                        elif g % 2 == 0:
                            dve.wait_ge(bc_in[q][load], bc_loaded(q, load, i))
                        if not (first and q == 0 and g < RING):
                            dve.wait_ge(p1_used, NG * p + g + 1 - RING)
                        nc.vector.tensor_tensor(ring[:, g % RING, :, :], x0_chunks(q, GC * g, GC), x1_bc,
                                                ALU.mult).then_inc(p1_ready, 1)
                    if not (last and q == 1):
                        layer0(p + 1, 1 - q, i + 1, first and q == 0)
                    dve.wait_ge(x2_ready, p + 1)
                    for g in L2_ORDER:
                        if g in P2_POOL:
                            continue
                        chunk = x0_chunks(q, GC * g, GC)
                        nc.vector.tensor_tensor(chunk, chunk, x2_bc, ALU.mult).then_inc(p2_dve, 1)

            def spread_chunk(c):
                if c % LC == 0:
                    wait_first_fields(dve, c // LC)
                if c == BY_LAYER0:
                    dve.wait_ge(one_hot_ready, len(looked))
                before = [b for b in range(c) if spread_place(b) is spread_place(c)]
                if before:
                    dve.wait_ge(chunk_placed, 2 * before[-1] + 2)
                nc.vector.tensor_copy(spread_place(c),
                                      gath_first.rearrange("p (m d) -> p m d", d=D)[:, 2 * c:2 * c + 2, 0:DP]
                                      .unsqueeze(2).broadcast_to([P, 2, P // 2, DP])).then_inc(chunk_spread, 1)

            dve.wait_ge(row_no_in, 16)
            dve.wait_ge(ids_first_in, 16)
            for k, f in enumerate(looked):
                c = k - LOOK_AHEAD
                if 0 <= c < BY_LOOKUPS:
                    spread_chunk(c)
                n = table_rows[f] // LP
                if k >= ONE_HOTS:
                    dve.wait_ge(lookup_mm, k + 1 - ONE_HOTS)
                first_no = sum(m for m in {table_rows[g] // LP for g in looked} if m > n)
                nc.vector.tensor_tensor(one_hot[k % ONE_HOTS][:, 0:n, :],
                                        ids_bc[:, P * k:P * k + P].unsqueeze(1).broadcast_to([LP, n, P]),
                                        row_no_sb[:, first_no:first_no + n].unsqueeze(2).broadcast_to([LP, n, P]),
                                        ALU.is_equal).then_inc(one_hot_ready, 1)
            spread_chunk(BY_LOOKUPS)
            dve.wait_ge(w0_in, 16)
            dve.wait_ge(w0b_in, 16)
            for rows, cs in ((slice(0, 2 * M), slice(0, 1)), (slice(2 * M, 3 * M), slice(0, 1)),
                             (slice(0, P), slice(1, N0)), (slice(0, HALF), slice(N0, N0 + 1))):
                last = nc.vector.tensor_tensor(w0_sb[rows, cs, :], w0_sb[rows, cs, :], w0_bwd_sb[rows, cs, :], ALU.add)
            last.then_inc(w0_sym, 1)
            dve.wait_ge(w0_sym, 1)
            g_first = gath_first.rearrange("p (m d) -> p m d", d=D)
            early = M - M // NL
            for g in range(NL - 1):
                wait_first_fields(dve, g)
            for jj in range(4):
                nc.vector.tensor_copy(fields_rep[:, M * jj:M * jj + early - jj, :], g_first[:, jj:early, 0:DP])
                if jj:
                    nc.vector.tensor_copy(fields_rep[:, M * jj + M - jj:M * jj + M, :], g_first[:, 0:jj, 0:DP])
            wait_first_fields(dve, NL - 1)
            for jj in range(4):
                last = nc.vector.tensor_copy(fields_rep[:, M * jj + early - jj:M * jj + M - jj, :],
                                             g_first[:, early:M, 0:DP])
            last.then_inc(rep_ordered, 1)
            for c in range(BY_LAYER0, LC * PLACED):
                spread_chunk(c)
            dve.wait_ge(x0rep_ready, 1)
            for c, (rows, ps) in enumerate(FIRST_ROWS):
                dve.wait_ge(rows_placed, c + 2)
                nc.vector.tensor_tensor(rot[0:rows, c, :], x0rep[0][0:rows, :], ps[0:rows, :],
                                        ALU.mult).then_inc(p0_dve, 1)
            dve.wait_ge(p0_used, 1)
            for half in range(2):
                last = nc.vector.tensor_scalar(x1_ps[64 * half:64 * half + 64, TILE:PAIR], acc[0][64:128, :],
                                               0.0, None, ALU.max)
            last.then_inc(x1_b_ready, 1)
            dve.wait_ge(x1_b_ready, 1)
            two_pairs(0, True, False)
            with dve.Fori(1, NB - 1) as i:
                two_pairs(i, False, False)
            two_pairs(NB - 1, False, True)
            r = relu_z[2]
            dve.wait_ge(acc_read, 3 * NP)
            nc.vector.tensor_tensor(r[:, 0:256], r[:, 0:256], r[:, 256:512], ALU.add).then_inc(z_last, 1)
            dve.wait_ge(z_last, 1)
            nc.vector.tensor_tensor(r[:, 0:128], r[:, 0:128], r[:, 128:256], ALU.add).then_inc(z_last, 1)
            dve.wait_ge(z_last, 2)
            dve.wait_ge(z_added[2], NP - 1)
            nc.vector.tensor_tensor(z[2][:], z[2][:], r[:, 0:128], ALU.add).then_inc(z_added[2], 1)

        @block.tensor
        def _(pe):
            def both(bank, w, prod, start, stop):
                for t in range(2):
                    last = nc.tensor.matmul(bank[64 * t:64 * t + 64, :], w, prod[:, TILE * t:TILE * t + TILE],
                                            start=start, stop=stop)
                return last

            def transpose_x0(q, g):
                for n in range(DP):
                    last = nc.tensor.transpose(aux[0:M, P * n:P * n + P],
                                               g.rearrange("p (m d) -> p m d", d=D)[:, :, DP * q + n], ident[:])
                last.then_inc(transposed, 1)

            def layer0(pair, bank, every):
                for c in range(N0):
                    if c % 2 == 0:
                        pe.wait_ge(p0_dve, p0_dve_done(pair, c // 2 + 1))
                    both(bank, w0_sb[:, c, :], rot[:, c, :], c == 0, False)
                if every:
                    pe.wait_ge(p0_dve, p0_dve_done(pair, 3))
                else:
                    pe.wait_ge(p0_pool, pair - 1)
                both(bank, w0_sb[0:HALF, N0, :], rot[0:HALF, N0, :], False, True).then_inc(p0_used, 1)

            def fold_z01(block_):
                for l in range(2):
                    pe.wait_ge(z_added[l], 2 * (block_ + 1))
                    last = nc.tensor.matmul(aux[K * l:K * l + K, 0:P], fold_sb[:], z[l][:], start=True, stop=True)
                last.then_inc(z_folded, 1)

            def fold_z2(block_):
                col = fold_col(block_)
                pe.wait_ge(z_added[2], 2 * (block_ + 1))
                pe.wait_ge(mlp_in_ready, 2 * block_ + 1)
                if col == TILE:
                    pe.wait_ge(y_ready, NB - 1)
                nc.tensor.matmul(aux[0:K, col:col + P], fold_sb[:], z[2][:], start=True, stop=True).then_inc(z_folded, 1)

            def keep_busy(n, bank):
                for _ in range(n):
                    nc.tensor.matmul(bank[:, 0:P], ident[:], ident[:], start=True, stop=True)

            def mlp_h1(block_):
                for n, x in enumerate((mlp_in_01, mlp_in_2d)):
                    if n == 0 and fold_col(block_) == TILE:
                        pe.wait_ge(mlp_in_ready, 2 * block_ + 1)
                    else:
                        pe.wait_ge(mlp_in_ready, 2 * block_ + 2)
                    if n == 1:
                        pe.wait_ge(dense_in, 16 * (block_ + 1))
                    for c in range(C1):
                        last = nc.tensor.matmul(aux[:, P * c:P * c + P], wt1_sb[0:x.shape[0], n, P * c:P * c + P], x[:],
                                                start=(n == 0 and c == 0), stop=(n == 1), skip_group_check=True)
                    if n == 0 and fold_col(block_) == TILE:
                        pe.wait_ge(acc_read, 3 * NP - 2)
                        keep_busy(6, acc[0])
                        fold_z2(block_)
                        keep_busy(3, acc[0])
                last.then_inc(h1_mm, 1)

            def mlp_h2(block_):
                for c in range(C1):
                    pe.wait_ge(h1_ready, C1 * block_ + c + 1)
                    for n in range(C2):
                        last = nc.tensor.matmul(aux[:, TILE + P * n:TILE + P * n + P], wt2_sb[:, c, P * n:P * n + P],
                                                h1[:, c, :], start=(c == 0 and n == 0), stop=(c == C1 - 1),
                                                skip_group_check=True)
                last.then_inc(h2_mm, 1)

            def mlp_y(block_):
                pe.wait_ge(h2_ready, block_ + 1)
                for c in range(C2):
                    last = nc.tensor.matmul(aux[:, TILE + 256:TILE + 257], h2[:, c, :], wt3_sb[:, c:c + 1],
                                            start=(c == 0), stop=(c == C2 - 1))
                last.then_inc(y_mm, 1)

            def layer2(i, q, begin, end, bank, first, last):
                p = 2 * i + q
                for n in range(begin, end):
                    g = L2_ORDER[n]
                    if n == T_AT[0] and q == 0 and not last:
                        pe.wait_ge(gathered, 16 * M * (i + 1))
                        if not first:
                            pe.wait_ge(h1_ready, C1 * i)
                        transpose_x0(0, gath[:])
                    if n == T_AT[1] and q == 0 and not last:
                        pe.wait_ge(x0rep_ready, 2 * i + 3)
                        transpose_x0(1, gath[:])
                    if n == FOLD_AT[1] and q == 1 and last:
                        fold_z01(i)
                    if g in P2_POOL:
                        pe.wait_ge(p2_pool, GC * (len(P2_POOL) * p + P2_POOL.index(g) + 1))
                    else:
                        pe.wait_ge(p2_dve, P2_DVE * p + [k for k in L2_ORDER if k not in P2_POOL].index(g) + 1)
                    for c in range(GC):
                        done = both(bank, w2_sb[:, GC * g + c, :], x0_chunks(q, GC * g + c, 1)[:, 0, :],
                                    n == 0 and c == 0, n == NG - 1 and c == GC - 1)
                    if (n + 1) * GC % LC == 0:
                        done.then_inc(p2_used, 1)

            def two_pairs(i, first, last):
                for q in range(2):
                    p = 2 * i + q
                    bank, other = acc[(3 * q + 1) % 2], acc[(3 * q + 2) % 2]
                    if not (first and q == 0):
                        pe.wait_ge(acc_read, 3 * p)
                    for g in range(NG):
                        if q == 0 and not first and g == FOLD_AT[0]:
                            pe.wait_ge(x0rep_ready, 2 * i + 2)
                            fold_z01(i - 1)
                        if q == 0 and not first and g == FOLD_AT[1]:
                            fold_z2(i - 1)
                        pe.wait_ge(p1_ready, NG * p + g + 1)
                        for c in range(GC):
                            done = both(bank, w1_sb[:, GC * g + c, :], ring[:, g % RING, c, :],
                                        g == 0 and c == 0, g == NG - 1 and c == GC - 1)
                        done.then_inc(p1_used, 1)
                    if q == 0 and not first:
                        mlp_h1(i - 1)
                    if q == 1 and not first:
                        if not last:
                            pe.wait_ge(x0rep_ready, 2 * i + 4)
                        mlp_h2(i - 1)
                    if not (last and q == 1):
                        pe.wait_ge(acc_read, 3 * p + 1)
                        layer0(p + 1, other, first and q == 0)
                    if last and q == 1:
                        layer2(i, 0, NG - DEFERRED, NG, acc[1], first, last)
                        layer2(i, 1, 0, NG, x1_ps[:, 0:TILE], first, last)
                    else:
                        pe.wait_ge(acc_read, 3 * p + 2)
                        layer2(i, q, 0, NG - DEFERRED if last else NG, bank, first, last)
                    if q == 1 and not first:
                        mlp_y(i - 1)

            def place(ps, rows):
                for d in range(DP):
                    last = nc.tensor.transpose(ps[0:rows.shape[1], P * d:P * d + P], rows[:, :, d], ident[:])
                last.then_inc(rows_placed, 1)

            def place_rot(c):
                rows, ps = FIRST_ROWS[c]
                first = 4 * c + 3 if c < N0 else HALF
                place(ps, fields_round.rearrange("p a m d -> p (a m) d")[:, first:first + rows, :])

            def layer0_first(c):
                rows = FIRST_ROWS[c][0]
                pe.wait_ge(p0_dve, p0_dve_done(0, c + 1))
                done = both(acc[0], w0_sb[0:rows, c, :], rot[0:rows, c, :], c == 0, c == N0)
                if c == N0:
                    done.then_inc(p0_used, 1)

            def place_chunk(c):
                rows = spread_place(c).rearrange("p a r d -> p (a r) d")
                pe.wait_ge(chunk_spread, c + 1)
                for t in range(2):
                    if c:
                        pe.wait_ge(chunk_copied, 2 * c + t - 1)
                    for d in range(DP // 2 * t, DP // 2 * (t + 1)):
                        last = nc.tensor.transpose(aux[:, P * d:P * d + P], rows[:, :, d], ident[:])
                    last.then_inc(chunk_placed, 1)

            pe.wait_ge(ident_in, 16)
            keep_busy(WARM_UP, aux)
            pe.wait_ge(small_in, 16)
            col = 0
            for k, f in enumerate(looked):
                c = k - LOOK_AHEAD
                if 0 <= c < BY_LOOKUPS:
                    place_chunk(c)
                pe.wait_ge(one_hot_ready, k + 1)
                n = table_rows[f] // LP
                j, m = k // LQ, k % LQ
                if m == 0 and j >= 3:
                    pe.wait_ge(lookup_copied, j - 2)
                for r in range(n):
                    last = nc.tensor.matmul(lookup_ps[j % 3][32 * m:32 * m + 32, :],
                                            small_sb[:, col + D * r:col + D * r + 32], one_hot[k % ONE_HOTS][:, r, :],
                                            start=(r == 0), stop=(r == n - 1))
                last.then_inc(lookup_mm, 1)
                if m == LQ - 1 or k == len(looked) - 1:
                    if j >= 2:
                        pe.wait_ge(looked_up, LQ * (j - 1))
                    pe.wait_ge(lookup_copied, j + 1)
                    nc.tensor.transpose(lookup_t_ps[j % 2][:, 0:32 * m + 32], lookup_sb[j % 2][0:32 * m + 32, :],
                                        ident[0:32 * m + 32, 0:32 * m + 32]).then_inc(lookup_t, 1)
                col += D * n
            for c in range(BY_LOOKUPS, BY_LAYER0):
                place_chunk(c)
            keep_busy(7, acc[0])
            pe.wait_ge(rep_ordered, 1)
            pe.wait_ge(chunk_copied, 2 * BY_LAYER0)
            place(aux, fields_rep)
            pe.wait_ge(round_ordered, 1)
            place_rot(0)
            place_rot(1)
            pe.wait_ge(w0_in, 16)
            pe.wait_ge(w0_sym, 1)
            for c in range(2, N0 + 1):
                if c == 2:
                    pe.wait_ge(x0rep_ready, 1)
                else:
                    pe.wait_ge(p0_dve, c - 2)
                place_rot(c)
                layer0_first(c - 2)
            layer0_first(N0 - 1)
            layer0_first(N0)
            transpose_x0(1, gath_first)
            keep_busy(6, acc[1])
            pe.wait_ge(x0rep_ready, 2)
            for c in range(BY_LAYER0, LC * PLACED):
                place_chunk(c)
            pe.wait_ge(w1_in, 16)
            pe.wait_ge(w2_in, 16)
            pe.wait_ge(mlp_in, 7 * 16)
            two_pairs(0, True, False)
            with pe.Fori(1, NB - 1) as i:
                two_pairs(i, False, False)
            two_pairs(NB - 1, False, True)
            mlp_h1(NB - 1)
            keep_busy(4, acc[0])
            mlp_h2(NB - 1)
            mlp_y(NB - 1)


def layer0_rows():
    part, chunk = np.meshgrid(np.arange(P), np.arange(N0 + 1), indexing="ij")
    m = part % M
    a = np.where(chunk < N0, m + part // M, m) % M
    b = np.where(chunk < N0, m + 4 * chunk + 3, m + HALF) % M
    return M * a + b, M * b + a


def row_numbers(ns):
    return np.concatenate([n * np.arange(LP)[:, None] + np.arange(n)[None, :] for n in ns], axis=1).astype(np.int32)


def kernel(**inputs):
    import concourse.bacc as bacc
    from concourse.bass_utils import run_bass_kernel_spmd

    fwd, bwd = layer0_rows()
    w0 = np.asarray(inputs["L0_rec_W0"]).reshape(M * M, K)
    ids = np.asarray(inputs["ids"])
    tables = [np.asarray(inputs[f"tbl_{f}"]) for f in range(M)]
    looked = looked_up_fields([t.shape[0] for t in tables])
    arrays = {
        "ids_first": np.ascontiguousarray(ids[0:P, looked].T),
        "small_tables": np.concatenate([tables[f].reshape(LP, -1) for f in looked]
                                       + [np.zeros((LP, 32 - D), np.float32)], axis=1),
        "row_no": row_numbers(sorted({tables[f].shape[0] // LP for f in looked}, reverse=True)),
        "dense_t": np.ascontiguousarray(np.asarray(inputs["dense_ctx"]).T),
        "ids": np.ascontiguousarray(inputs["ids"]),
        "w0_fwd": np.ascontiguousarray(w0[fwd]),
        "w0_bwd": np.ascontiguousarray(w0[bwd]),
        "w1": np.ascontiguousarray(inputs["L0_rec_W1"]),
        "w2": np.ascontiguousarray(inputs["L0_rec_W2"]),
        "w_top1": np.ascontiguousarray(inputs["W_top1"]),
        "b_top1": np.ascontiguousarray(np.asarray(inputs["b_top1"]).reshape(-1, P).T),
        "w_top2": np.ascontiguousarray(inputs["W_top2"]),
        "b_top2": np.ascontiguousarray(np.asarray(inputs["b_top2"]).reshape(-1, P).T),
        "w_top3": np.ascontiguousarray(np.asarray(inputs["W_top3"]).reshape(-1, P).T),
        "eye": np.eye(P, dtype=np.float32),
        "fold": np.tile(np.eye(K, dtype=np.float32), (2, 1)),
    }
    for f in range(M):
        arrays[f"tbl_{f}"] = np.ascontiguousarray(inputs[f"tbl_{f}"])

    nc = bacc.Bacc("TRN2", target_bir_lowering=False, num_devices=1)
    ap = {n: nc.dram_tensor(n, a.shape, mybir.dt.from_np(a.dtype), kind="ExternalInput").ap()
          for n, a in arrays.items()}
    y = nc.dram_tensor("y", (arrays["ids"].shape[0], 1), F32, kind="ExternalOutput").ap()
    build(nc, ap["fold"], ap["ids_first"], ap["small_tables"], ap["row_no"], ap["dense_t"], ap["ids"],
          [ap[f"tbl_{f}"] for f in range(M)], ap["w0_fwd"], ap["w0_bwd"], ap["w1"], ap["w2"], ap["w_top1"],
          ap["b_top1"], ap["w_top2"], ap["b_top2"], ap["w_top3"], ap["eye"], y)
    r = run_bass_kernel_spmd(nc, [arrays], core_ids=[0])
    return r.results[0]["y"]
```
